# Optimizing a Trainium2 kernel written in Bass

```python
import numpy as np
import jax
import jax.numpy as jnp

def _softmax(x, axis=-1):
    return jax.nn.softmax(x, axis=axis)

def _gelu(x):
    return jax.nn.gelu(x, approximate=True)

def _silu(x):
    return jax.nn.silu(x)

def _sigmoid(x):
    return jax.nn.sigmoid(x)

def _layernorm(x, axis=-1, eps=1e-05):
    m = jnp.mean(x, axis=axis, keepdims=True)
    v = jnp.var(x, axis=axis, keepdims=True)
    return (x - m) / jnp.sqrt(v + eps)

def _scatter_add(tgt, idx, src, axis=0):
    return tgt.at[idx].add(src)

def _segment_sum(src, seg, n):
    return jax.ops.segment_sum(src, seg, n)
kernel_name = 'mk_seq_preln_d1_jaxref_r8_bb622b'

def setup_inputs(seed: int=0):
    np.random.seed(seed)
    _w = jnp.asarray

    def _L0_attn_setup():
        import jax, jax.numpy as jnp
        import numpy as np
        B, S, D, H = (4, 256, 128, 16)
        HD = D // H
        LN_EPS = 1e-05
        KERN_EPS = 1e-06

        def kernel_func(q, k):
            scores = jnp.einsum('bhqd,bhkd->bhqk', q, k) / jnp.sqrt(jnp.asarray(HD, q.dtype))
            w = jax.nn.relu(scores)
            return w / (jnp.sum(w, axis=-1, keepdims=True) + KERN_EPS)
        key = jax.random.key(seed)
        k1, k2, k3 = jax.random.split(key, 3)
        scale = 1.0 / np.sqrt(D)
        return {'x': jax.random.normal(k1, (B, S, D), dtype=jnp.float32), 'w_qkv': jax.random.normal(k2, (D, 3 * D), dtype=jnp.float32) * scale, 'w_out': jax.random.normal(k3, (D, D), dtype=jnp.float32) * scale, 'b_out': jnp.zeros((D,), dtype=jnp.float32), 'gamma': jnp.ones((D,), dtype=jnp.float32), 'beta': jnp.zeros((D,), dtype=jnp.float32)}
    _L0_attn_in = _L0_attn_setup()

    def _L0_ffn_setup():
        import jax, jax.numpy as jnp
        import numpy as np
        INPUT_SIZE = 128
        OUTPUT_SIZE = 128
        key = jax.random.key(seed)
        kx, kt, kp, ktn, kpn = jax.random.split(key, 5)
        x = jax.random.normal(kx, (8, 256, INPUT_SIZE), dtype=jnp.float32)
        theta = jax.random.normal(kt, (INPUT_SIZE, OUTPUT_SIZE), dtype=jnp.float32) * 0.02
        phi = jax.random.normal(kp, (INPUT_SIZE, OUTPUT_SIZE), dtype=jnp.float32) * 0.02
        theta_noise = jax.random.normal(ktn, (INPUT_SIZE, OUTPUT_SIZE), dtype=jnp.float32) * 0.01
        phi_noise = jax.random.normal(kpn, (INPUT_SIZE, OUTPUT_SIZE), dtype=jnp.float32) * 0.01
        return {'x': x, 'theta': theta, 'phi': phi, 'theta_noise': theta_noise, 'phi_noise': phi_noise}
    _L0_ffn_in = _L0_ffn_setup()
    _d = {'L0_attn_x': _L0_attn_in['x'], 'L0_attn_w_qkv': _L0_attn_in['w_qkv'], 'L0_attn_w_out': _L0_attn_in['w_out'], 'L0_attn_b_out': _L0_attn_in['b_out'], 'L0_attn_gamma': _L0_attn_in['gamma'], 'L0_attn_beta': _L0_attn_in['beta'], 'L0_ffn_theta': _L0_ffn_in['theta'], 'L0_ffn_phi': _L0_ffn_in['phi'], 'L0_ffn_theta_noise': _L0_ffn_in['theta_noise'], 'L0_ffn_phi_noise': _L0_ffn_in['phi_noise']}
    _x0 = _d['L0_attn_x']
    _d['L0_attn_x'] = jax.random.normal(jax.random.fold_in(jax.random.key(seed), 1), (1, 2048, 128), dtype=_x0.dtype)
    del _x0
    return _d

def reference(L0_attn_x, L0_attn_w_qkv, L0_attn_w_out, L0_attn_b_out, L0_attn_gamma, L0_attn_beta, L0_ffn_theta, L0_ffn_phi, L0_ffn_theta_noise, L0_ffn_phi_noise):

    def _L0_attn_ref(x, w_qkv, w_out, b_out, gamma, beta):
        import jax, jax.numpy as jnp
        import numpy as np
        B, S, D, H = (4, 256, 128, 16)
        HD = D // H
        LN_EPS = 1e-05
        KERN_EPS = 1e-06

        def kernel_func(q, k):
            scores = jnp.einsum('bhqd,bhkd->bhqk', q, k) / jnp.sqrt(jnp.asarray(HD, q.dtype))
            w = jax.nn.relu(scores)
            return w / (jnp.sum(w, axis=-1, keepdims=True) + KERN_EPS)
        Bx, Sx, _ = x.shape
        qkv = (x @ w_qkv).reshape(Bx, Sx, H, 3 * HD)
        q, k, v = jnp.split(qkv, 3, axis=-1)
        q = q.transpose(0, 2, 1, 3)
        k = k.transpose(0, 2, 1, 3)
        v = v.transpose(0, 2, 1, 3)
        attn = kernel_func(q, k)
        out = jnp.einsum('bhqk,bhkd->bhqd', attn, v)
        out = out.transpose(0, 2, 1, 3).reshape(Bx, Sx, D)
        out = out @ w_out + b_out
        y = x + out
        mu = jnp.mean(y, axis=-1, keepdims=True)
        var = jnp.var(y, axis=-1, keepdims=True)
        return (y - mu) * jax.lax.rsqrt(var + LN_EPS) * gamma + beta

    def _L0_ffn_ref(x, theta, phi, theta_noise, phi_noise):
        import jax, jax.numpy as jnp
        import numpy as np
        INPUT_SIZE = 128
        OUTPUT_SIZE = 128
        real = jnp.einsum('bti,io->bto', x, jnp.cos(theta + theta_noise))
        imag = jnp.einsum('bti,io->bto', x, jnp.sin(phi + phi_noise))
        return jnp.sqrt(real * real + imag * imag)
    x = L0_attn_x
    x = x + _L0_attn_ref(_layernorm(x, axis=-1), L0_attn_w_qkv, L0_attn_w_out, L0_attn_b_out, L0_attn_gamma, L0_attn_beta)
    x = x + _L0_ffn_ref(_layernorm(x, axis=-1), L0_ffn_theta, L0_ffn_phi, L0_ffn_theta_noise, L0_ffn_phi_noise)
    return x

_drawn_inputs = setup_inputs


def setup_inputs(seed=0):
    import zlib

    import numpy as np

    out = dict(_drawn_inputs(seed))
    spreads = {'L0_attn_b_out': (0.0, 0.1), 'L0_attn_gamma': (1.0, 0.2), 'L0_attn_beta': (0.0, 0.1)}
    factors = {'L0_ffn_theta': 8.0, 'L0_ffn_theta_noise': 8.0}
    for name, (base, spread) in spreads.items():
        noise = np.random.default_rng([zlib.crc32(name.encode()), seed]).standard_normal(out[name].shape)
        drawn = base * np.exp(spread * noise) if base else spread * noise
        out[name] = jnp.asarray(drawn.astype(out[name].dtype))
    for name, factor in factors.items():
        out[name] = (out[name] * factor).astype(out[name].dtype)
    return out
```

```python
import math
from contextlib import ExitStack

import concourse.bass as bass
from concourse import mybir

F32 = mybir.dt.float32
F32R = mybir.dt.float32r
ALU = mybir.AluOpType
ACT = mybir.ActivationFunctionType

P = 128
S, D, H = 2048, 128, 16
HD = D // H
NT = S // P
TPC = 4
NC = NT // TPC
CW = TPC * P
G = 4
HPG = H // G
VW = 32
STEPS = G * NT
PSUM_PAIRS = 3
LN_EPS = 1e-5
DEN_EPS = 1e-6 * math.sqrt(HD)
TWO_PI = 2 * math.pi
ROUND = 1.5 * 2.0**23
TWO_PI_PARTS = (6.28125, 0.0019340515136718750, TWO_PI - 6.28125 - 0.0019340515136718750)
PI_BELOW = 3.1415925
NORM_SEQ = 2
POST_SEQ = 6


class Own:

    def __init__(self, engine, sem, base=0):
        self.engine, self.sem, self.base, self.n = engine, sem, base, 0

    def __call__(self, instruction):
        self.n += 1
        instruction.then_inc(self.sem, 1)
        self.engine.wait_ge(self.sem, self.base + self.n)


def block_kernel(nc, x, w_qkv, w_out, b_out, gamma, beta, theta, phi, theta_noise, phi_noise, out):
    x_v = x.rearrange("o (p t) d -> p (o t) d", p=P)
    out_v = out.rearrange("o (p t) d -> p (o t) d", p=P)
    ctx = ExitStack()
    with ctx:
        def sb(name, shape, dt=F32):
            return ctx.enter_context(nc.sbuf_tensor(name, shape, dt))

        def sem(name):
            return ctx.enter_context(nc.semaphore(name))

        ident = sb("ident", [P, P])
        x_sb = sb("x_sb", [P, NT, D])
        xn = sb("xn", [P, NT, D])
        x_beta = sb("x_beta", [P, NT, D])
        xT = sb("xT", [P, NT * P])
        wqkv_sb = sb("wqkv_sb", [P, 3 * D])
        w3 = sb("w3", [P, 3, D])
        wout_sb = sb("wout_sb", [P, D])
        bout_b = sb("bout_b", [P, D])
        gamma_b = sb("gamma_b", [P, D])
        beta_b = sb("beta_b", [P, D])
        k_hi = sb("k_hi", [P, S], F32R)
        k_lo = sb("k_lo", [P, S], F32R)
        q_hi = sb("q_hi", [P, S], F32R)
        q_lo = sb("q_lo", [P, S], F32R)
        k_rep = sb("k_rep", [P, G, S], F32R)
        q_rep = sb("q_rep", [P, G, CW], F32R)
        v_sb = sb("v_sb", [P, NT, H, VW])
        w_buf = sb("w_buf", [P, 3, HPG, CW])
        pv_sb = sb("pv_sb", [P, CW])
        den = sb("den", [P, TPC, HPG])
        o_sb = sb("o_sb", [P, TPC, D])
        oT = sb("oT", [P, CW])
        y = sb("y", [P, TPC, D])
        z = sb("z", [P, TPC, D])
        x1 = sb("x1", [P, TPC, D])
        x1n = sb("x1n", [P, TPC, D])
        x1T = sb("x1T", [P, CW])
        sq = sb("sq", [P, 2, CW])
        x2 = sb("x2", [P, TPC, D])
        angles = sb("angles", [P, 4, D])
        turns = sb("turns", [P, 2, D])
        ffn_w = sb("ffn_w", [P, 2, D])
        stats = sb("stats", [P, NT, 6])
        mv = sb("mv", [P, NT, 2])
        inv_var = sb("inv_var", [P, NT])
        rstd = sb("rstd", [P, NT])
        stats_p = sb("stats_p", [P, TPC, 6])
        mv_p = sb("mv_p", [P, TPC, 2])
        iv_p = sb("iv_p", [P, TPC])
        spare = sb("spare", [P, 1])
        rs_p = sb("rs_p", [P, TPC])

        sc = [ctx.enter_context(nc.psum_tensor(f"sc{i}", [P, 2, CW], F32)) for i in range(PSUM_PAIRS)]
        pv = [ctx.enter_context(nc.psum_tensor(f"pv{i}", [P, CW], F32)) for i in range(2)]

        x_loaded = [sem(f"x_loaded{c}") for c in range(NC)]
        wqkv_loaded = sem("wqkv_loaded")
        consts_loaded = sem("consts_loaded")
        angles_loaded = sem("angles_loaded")
        ident_zero = sem("ident_zero")
        ident_ready = sem("ident_ready")
        w3_ready = sem("w3_ready")
        v_pad = sem("v_pad")
        ln_own = sem("ln_own")
        var_ready = sem("var_ready")
        rstd_ready = sem("rstd_ready")
        xn_ready = sem("xn_ready")
        xT_done = sem("xT_done")
        xT_ready = sem("xT_ready")
        k_done = sem("k_done")
        q_done = sem("q_done")
        v_done = sem("v_done")
        k_hi_ready = sem("k_hi_ready")
        k_lo_ready = sem("k_lo_ready")
        q_hi_ready = sem("q_hi_ready")
        q_lo_ready = sem("q_lo_ready")
        v_ready = sem("v_ready")
        k0_loaded = [sem(f"k0_loaded{c}") for c in range(NC)]
        k_loaded = [None] + [sem(f"k_loaded{g}") for g in range(1, G)]
        q_loaded = [sem(f"q_loaded{g}") for g in range(G)]
        xb_ready = sem("xb_ready")
        trig_own = sem("trig_own")
        angles_ready = sem("angles_ready")
        ffn_w_ready = sem("ffn_w_ready")
        scores = [sem("scores_act"), sem("scores_dve")]
        relu = [sem("relu_act"), sem("relu_dve")]
        pv_done = sem("pv_done")
        pv_out = sem("pv_out")
        pvT_done = sem("pvT_done")
        norm_own = sem("norm_own")
        normed = sem("normed")
        oT_done = sem("oT_done")
        oT_ready = sem("oT_ready")
        proj_done = sem("proj_done")
        post_own = sem("post_own")
        y_ready = sem("y_ready")
        iv_ready = sem("iv_ready")
        rs_ready = sem("rs_ready")
        z_ready = sem("z_ready")
        z_own = sem("z_own")
        x1_ready = sem("x1_ready")
        x1n_ready = sem("x1n_ready")
        x1T_done = sem("x1T_done")
        x1T_ready = sem("x1T_ready")
        real_done = sem("real_done")
        imag_done = sem("imag_done")
        sq_ready = sem("sq_ready")
        sum_ready = sem("sum_ready")
        abs_ready = sem("abs_ready")
        x2_ready = sem("x2_ready")
        stored = sem("stored")

        def chunk(c):
            return bass.ds(c * TPC, TPC)

        def row(v, d):
            return v[:, :].unsqueeze(1).to_broadcast([P, d, D])

        with nc.Block() as block:
            @block.sync
            def _(sp):
                def replicate_q(c, g):
                    for j in range(4):
                        src = q_lo if j % 2 else q_hi
                        sp.dma_start(
                            q_rep[j:P:4, g, :].bitcast(F32),
                            src[32 * g:32 * g + 32, bass.ds(c * CW, CW)].bitcast(F32),
                        ).then_inc(q_loaded[g], 16)

                def replicate_k(g, lo, n, done):
                    for j in range(4):
                        src = k_lo if j // 2 else k_hi
                        sp.dma_start(
                            k_rep[j:P:4, g, lo:lo + n].bitcast(F32),
                            src[32 * g:32 * g + 32, lo:lo + n].bitcast(F32),
                        ).then_inc(done, 16)

                def store(c):
                    sp.wait_ge(x2_ready, c + 1)
                    sp.dma_start(out_v[:, chunk(c), :], x2[:, :, :]).then_inc(stored, 16)

                def next_queries(c, g):
                    if isinstance(c, int):
                        sp.wait_ge(q_lo_ready, c + 2)
                    for s in scores:
                        sp.wait_ge(s, STEPS * c + NT * (g + 1))
                    replicate_q(c + 1, g)

                sp.dma_start(x_sb[:, 0:TPC, :], x_v[:, 0:TPC, :]).then_inc(x_loaded[0], 16)
                sp.dma_start(wqkv_sb[:, :], w_qkv).then_inc(wqkv_loaded, 16)
                for c in range(1, NC):
                    sp.dma_start(x_sb[:, chunk(c), :], x_v[:, chunk(c), :]).then_inc(x_loaded[c], 16)
                for c in range(NC):
                    sp.wait_ge(k_hi_ready, c + 1)
                    sp.wait_ge(k_lo_ready, c + 1)
                    replicate_k(0, c * CW, CW, k0_loaded[c])
                    if c == 0:
                        sp.wait_ge(q_hi_ready, 1)
                        sp.wait_ge(q_lo_ready, 1)
                        replicate_q(0, 0)
                for g in range(1, G):
                    replicate_q(0, g)
                    replicate_k(g, 0, S, k_loaded[g])
                for dst, src in ((bout_b, b_out), (gamma_b, gamma), (beta_b, beta)):
                    sp.dma_start(dst[:, :], src.partition_broadcast(P)).then_inc(consts_loaded, 16)
                sp.dma_start(wout_sb[:, :], w_out).then_inc(consts_loaded, 16)
                for n, src in enumerate((theta, phi, theta_noise, phi_noise)):
                    sp.dma_start(angles[:, n, :], src).then_inc(angles_loaded, 16)

                for g in range(G):
                    next_queries(0, g)
                with sp.Fori(1, NC - 1) as c:
                    next_queries(c, 0)
                    next_queries(c, 1)
                    store(c - 1)
                    next_queries(c, 2)
                    next_queries(c, 3)
                store(NC - 2)
                store(NC - 1)
                sp.wait_ge(stored, 16 * NC)

            @block.gpsimd
            def _(pool):
                nc.gpsimd.memset(ident[:, :], 0.0).then_inc(ident_zero, 1)
                pool.wait_ge(ident_zero, 1)
                nc.gpsimd.affine_select(out=ident[:, :], in_=ident[:, :], compare_op=ALU.not_equal, fill=1.0,
                                        base=0, pattern=[[-1, P]], channel_multiplier=1).then_inc(ident_ready, 1)
                pool.wait_ge(wqkv_loaded, 16)
                for n in range(3):
                    src = wqkv_sb[:, :].rearrange("p (h c d) -> p c h d", h=H, c=3)[:, n]
                    nc.gpsimd.tensor_copy(w3[:, n, :].rearrange("p (h d) -> p h d", h=H), src).then_inc(w3_ready, 1)
                for g in range(G):
                    heads = slice(HPG * g, HPG * (g + 1))
                    nc.gpsimd.memset(v_sb[:, :, heads, HD + 1:VW], 0.0).then_inc(v_pad, 1)
                    nc.gpsimd.memset(v_sb[:, :, heads, HD:HD + 1], 1.0).then_inc(v_pad, 1)
                pool.wait_ge(consts_loaded, 64)
                pool.wait_ge(xn_ready, NC)
                pool.wait_ge(xT_done, NC)
                for c in range(NC):
                    nc.gpsimd.tensor_tensor(xn[:, chunk(c), :], xn[:, chunk(c), :], row(bout_b, TPC),
                                            ALU.add).then_inc(xb_ready, 1)
                    nc.gpsimd.tensor_tensor(x_beta[:, chunk(c), :], x_sb[:, chunk(c), :], row(beta_b, TPC),
                                            ALU.add).then_inc(xb_ready, 1)

                def post(c):
                    pool.wait_ge(z_ready, c + 1)
                    if not isinstance(c, int) or c > 0:
                        pool.wait_ge(x2_ready, c)
                    nc.gpsimd.tensor_tensor(y[:, :, :], z[:, :, :], row(gamma_b, TPC), ALU.mult).then_inc(z_own, 1)
                    pool.wait_ge(z_own, c + 1)
                    nc.gpsimd.tensor_tensor(x1[:, :, :], y[:, :, :], x_beta[:, chunk(c), :],
                                            ALU.add).then_inc(x1_ready, 1)
                    pool.wait_ge(sq_ready, 2 * c + 2)
                    nc.gpsimd.tensor_tensor(sq[:, 0, :], sq[:, 0, :], sq[:, 1, :], ALU.add).then_inc(sum_ready, 1)
                    pool.wait_ge(abs_ready, c + 1)
                    if not isinstance(c, int) or c > 0:
                        pool.wait_ge(stored, 16 * c)
                    nc.gpsimd.tensor_tensor(x2[:, :, :].rearrange("p t d -> p (t d)"), sq[:, 1, :],
                                            x1[:, :, :].rearrange("p t d -> p (t d)"),
                                            ALU.add).then_inc(x2_ready, 1)

                pool.wait_ge(xb_ready, 2 * NC)
                post(0)
                with pool.Fori(1, NC) as c:
                    post(c)

            @block.scalar
            def _(act):
                def root(c):
                    act.wait_ge(var_ready, c + 1)
                    nc.scalar.activation(rstd[:, chunk(c)], inv_var[:, chunk(c)], ACT.Sqrt).then_inc(rstd_ready, 1)

                root(0)
                for c in range(NC):
                    cols = slice(c * CW, (c + 1) * CW)
                    act.wait_ge(xT_done, c + 1)
                    nc.scalar.copy(xT[:, cols], sc[0][:, c % 2, :]).then_inc(xT_ready, 1)
                    if c + 1 < NC:
                        root(c + 1)
                    act.wait_ge(k_done, c + 1)
                    nc.scalar.copy(k_hi[:, cols], sc[1][:, c % 2, :]).then_inc(k_hi_ready, 1)
                    if c == 0:
                        act.wait_ge(q_done, 1)
                        nc.scalar.copy(q_hi[:, cols], pv[0][:, :]).then_inc(q_hi_ready, 1)
                    act.wait_ge(v_done, c + 1)
                    nc.scalar.copy(
                        v_sb[:, chunk(c), :, 0:HD],
                        sc[2][:, c % 2, :].rearrange("p (t h d) -> p t h d", t=TPC, h=H),
                    ).then_inc(v_ready, 1)

                def relu_step(c, s):
                    act.wait_ge(scores[0], STEPS * c + s + 1)
                    nc.scalar.activation(w_buf[:, s % 3, 0:2, :], sc[2 * s % PSUM_PAIRS][:, :, :],
                                         ACT.Relu).then_inc(relu[0], 1)

                def take_pv(m):
                    act.wait_ge(pv_done, m + 1)
                    if not isinstance(m, int) or m > 0:
                        act.wait_ge(pvT_done, m)
                    nc.scalar.copy(pv_sb[:, :], pv[1 if take_pv.odd else 0][:, :]).then_inc(pv_out, 1)

                def take_q(c):
                    act.wait_ge(q_done, c + 1)
                    nc.scalar.copy(q_hi[:, c * CW:(c + 1) * CW], pv[(c + 1) % 2][:, :]).then_inc(q_hi_ready, 1)

                def trig():
                    act.wait_ge(angles_ready, 1)
                    nc.scalar.activation(ffn_w[:, :, :], angles[:, 0:2, :], ACT.Sin).then_inc(ffn_w_ready, 1)

                def take_oT(j):
                    act.wait_ge(oT_done, j + 1)
                    nc.scalar.copy(oT[:, :], pv[1][:, :]).then_inc(oT_ready, 1)

                def post_root(j, n):
                    act.wait_ge(iv_ready, 2 * j + n + 1)
                    nc.scalar.activation(rs_p[:, :], iv_p[:, :], ACT.Sqrt).then_inc(rs_ready, 1)

                def take_x1T(j):
                    act.wait_ge(x1T_done, j + 1)
                    nc.scalar.copy(x1T[:, :], pv[0][:, :]).then_inc(x1T_ready, 1)

                def square(j, n):
                    act.wait_ge((real_done, imag_done)[n], j + 1)
                    if n == 0 and (not isinstance(j, int) or j > 0):
                        act.wait_ge(x2_ready, j)
                    nc.scalar.activation(sq[:, n, :], pv[0][:, :], ACT.Square).then_inc(sq_ready, 1)

                def magnitude(j):
                    act.wait_ge(sum_ready, j + 1)
                    nc.scalar.activation(sq[:, 1, :], sq[:, 0, :], ACT.Sqrt).then_inc(abs_ready, 1)

                def after_pass(j):
                    return [((0, 6), lambda: take_oT(j)), ((0, 11), lambda: post_root(j, 0)),
                            ((1, 3), lambda: post_root(j, 1)), ((1, 8), lambda: take_x1T(j)),
                            ((1, 10), lambda: square(j, 0)), ((1, 12), lambda: square(j, 1)),
                            ((1, 14), lambda: magnitude(j))]

                def run_pass(c, hooks):
                    for g in range(G):
                        for k in range(NT):
                            relu_step(c, NT * g + k)
                            if k == 1 and not (isinstance(c, int) and c == 0 and g == 0):
                                take_pv.odd = g % 2 == 0
                                take_pv(G * c + g - 1)
                            for at, hook in hooks:
                                if at == (g, k):
                                    hook()

                run_pass(0, [((1, 8), lambda: take_q(1)), ((2, 8), lambda: take_q(2)),
                             ((3, 8), lambda: take_q(3)), ((2, 12), trig)])
                with act.Fori(1, NC) as c:
                    run_pass(c, after_pass(c - 1))
                take_pv.odd = True
                take_pv(G * NC - 1)
                for _, hook in after_pass(NC - 1):
                    hook()

            @block.vector
            def _(dve):
                own = Own(dve, ln_own)

                def statistics(c):
                    dve.wait_ge(x_loaded[c], 16)
                    for t in range(c * TPC, (c + 1) * TPC):
                        last = nc.vector.bn_stats(stats[:, t, :], x_sb[:, t, :])
                    own(last)
                    for t in range(c * TPC, (c + 1) * TPC):
                        last = nc.vector.bn_aggr(mv[:, t, :], stats[:, t, :])
                    own(last)
                    own(nc.vector.tensor_scalar_add(inv_var[:, chunk(c)], mv[:, chunk(c), 1], LN_EPS))
                    nc.vector.reciprocal(inv_var[:, chunk(c)], inv_var[:, chunk(c)]).then_inc(var_ready, 1)

                def normalise_x(c):
                    dve.wait_ge(rstd_ready, c + 1)
                    for t in range(c * TPC, (c + 1) * TPC):
                        last = nc.vector.tensor_scalar(xn[:, t, :], x_sb[:, t, :], mv[:, t, 0:1], rstd[:, t:t + 1],
                                                       ALU.subtract, ALU.mult)
                    last.then_inc(xn_ready, 1)

                def low_part(lo, hi, hi_ready, lo_ready, c, bank):
                    cols = slice(c * CW, (c + 1) * CW)
                    dve.wait_ge(hi_ready, c + 1)
                    nc.vector.tensor_tensor(lo[:, cols], bank, hi[:, cols].bitcast(F32),
                                            ALU.subtract).then_inc(lo_ready, 1)

                statistics(0)
                normalise_x(0)
                statistics(1)
                for c in range(NC):
                    if c + 1 < NC:
                        normalise_x(c + 1)
                    low_part(k_lo, k_hi, k_hi_ready, k_lo_ready, c, sc[1][:, c % 2, :])
                    if c == 0:
                        low_part(q_lo, q_hi, q_hi_ready, q_lo_ready, 0, pv[0][:, :])
                    if c + 2 < NC:
                        statistics(c + 2)

                def relu_step(c, s):
                    dve.wait_ge(scores[1], STEPS * c + s + 1)
                    nc.vector.tensor_scalar(w_buf[:, s % 3, 2:4, :], sc[(2 * s + 1) % PSUM_PAIRS][:, :, :],
                                            0.0, None, ALU.max).then_inc(relu[1], 1)

                def normalise(m, bank, g):
                    own = Own(dve, norm_own, NORM_SEQ * m)
                    pvT = bank[:, :].rearrange("p (t i v) -> p t i v", t=TPC, i=HPG)
                    dve.wait_ge(pvT_done, m + 1)
                    own(nc.vector.tensor_scalar_add(den[:, :, :], pvT[:, :, :, HD], DEN_EPS))
                    own(nc.vector.reciprocal(den[:, :, :], den[:, :, :]))
                    if g == 0 and not (isinstance(m, int) and m == 0):
                        dve.wait_ge(oT_done, m // G if isinstance(m, int) else normalise.chunk)
                    nc.vector.tensor_tensor(
                        o_sb[:, :, 32 * g:32 * g + 32].rearrange("p t (i d) -> p t i d", i=HPG),
                        pvT[:, :, :, 0:HD], den[:, :, :].unsqueeze(3).to_broadcast([P, TPC, HPG, HD]),
                        ALU.mult).then_inc(normed, 1)

                def trig_angles():
                    own = Own(dve, trig_own)
                    dve.wait_ge(angles_loaded, 64)
                    own(nc.vector.tensor_tensor(angles[:, 0:2, :], angles[:, 0:2, :], angles[:, 2:4, :], ALU.add))
                    nc.vector.tensor_scalar(turns[:, 0, :], angles[:, 0, :], 1 / TWO_PI, 0.25, ALU.mult, ALU.add)
                    own(nc.vector.tensor_scalar(turns[:, 1, :], angles[:, 1, :], 1 / TWO_PI, None, ALU.mult))
                    own(nc.vector.tensor_scalar_add(turns[:, :, :], turns[:, :, :], ROUND))
                    own(nc.vector.tensor_scalar_add(turns[:, :, :], turns[:, :, :], -ROUND))
                    for part in TWO_PI_PARTS:
                        own(nc.vector.scalar_tensor_tensor(out=angles[:, 0:2, :], in0=turns[:, :, :], scalar=-part,
                                                           in1=angles[:, 0:2, :], op0=ALU.mult, op1=ALU.add))
                    own(nc.vector.tensor_scalar_add(angles[:, 0, :], angles[:, 0, :], math.pi / 2))
                    nc.vector.tensor_scalar(angles[:, 0:2, :], angles[:, 0:2, :], PI_BELOW, -PI_BELOW, ALU.min,
                                            ALU.max).then_inc(angles_ready, 1)

                class Post:

                    def __init__(self, j):
                        self.j = j
                        self.own = Own(dve, post_own, POST_SEQ * j)

                    def residual(self):
                        dve.wait_ge(proj_done, self.j + 1)
                        nc_y = nc.vector.tensor_tensor(y[:, :, :], pv[1][:, :].rearrange("p (t d) -> p t d", t=TPC),
                                                       xn[:, chunk(self.j), :], ALU.add)
                        nc_y.then_inc(y_ready, 1)
                        dve.wait_ge(y_ready, self.j + 1)

                    def stats(self, src):
                        for t in range(TPC):
                            last = nc.vector.bn_stats(stats_p[:, t, :], src[:, t, :])
                        self.own(last)
                        nc.vector.memset(spare[:, :], 0.0)
                        for t in range(TPC):
                            last = nc.vector.bn_aggr(mv_p[:, t, :], stats_p[:, t, :])
                        self.own(last)
                        self.own(nc.vector.tensor_scalar_add(iv_p[:, :], mv_p[:, :, 1], LN_EPS))
                        nc.vector.reciprocal(iv_p[:, :], iv_p[:, :]).then_inc(iv_ready, 1)

                    def scale(self, dst, src, n, done):
                        dve.wait_ge(rs_ready, 2 * self.j + n + 1)
                        for t in range(TPC):
                            last = nc.vector.tensor_scalar(dst[:, t, :], src[:, t, :], mv_p[:, t, 0:1],
                                                           rs_p[:, t:t + 1], ALU.subtract, ALU.mult)
                        last.then_inc(done, 1)

                    def first_stats(self):
                        self.stats(y)

                    def second_stats(self):
                        dve.wait_ge(x1_ready, self.j + 1)
                        self.stats(x1)

                def after_pass(j):
                    post = Post(j)
                    return [((0, 8), post.residual), ((0, 9), post.first_stats),
                            ((0, 12), lambda: post.scale(z, y, 0, z_ready)),
                            ((1, 1), post.second_stats),
                            ((1, 5), lambda: post.scale(x1n, x1, 1, x1n_ready))]

                def run_pass(c, hooks):
                    for g in range(G):
                        for k in range(NT):
                            relu_step(c, NT * g + k)
                            if k == 3 and not (isinstance(c, int) and c == 0 and g == 0):
                                normalise.chunk = c
                                normalise(G * c + g - 1, pv[(g + 1) % 2], (g - 1) % G)
                            for at, hook in hooks:
                                if at == (g, k):
                                    hook()

                def take_q(c):
                    low_part(q_lo, q_hi, q_hi_ready, q_lo_ready, c, pv[(c + 1) % 2][:, :])

                run_pass(0, [((1, 8), lambda: take_q(1)), ((2, 8), lambda: take_q(2)),
                             ((3, 8), lambda: take_q(3)), ((2, 5), trig_angles)])
                dve.wait_ge(xb_ready, 2 * NC)
                with dve.Fori(1, NC) as c:
                    run_pass(c, after_pass(c - 1))
                normalise(G * NC - 1, pv[1], G - 1)
                for _, hook in after_pass(NC - 1):
                    hook()

            @block.tensor
            def _(pe):
                def transpose_x(c):
                    pe.wait_ge(xn_ready, c + 1)
                    if c == 0:
                        pe.wait_ge(ident_ready, 1)
                    if c >= 2:
                        pe.wait_ge(xT_ready, c - 1)
                    for t in range(TPC):
                        last = nc.tensor.transpose(sc[0][:, c % 2, t * P:(t + 1) * P], xn[:, c * TPC + t, :],
                                                   ident[:, :])
                    last.then_inc(xT_done, 1)

                def project_q(c, bank):
                    nc.tensor.matmul(bank, w3[:, 0, :], xT[:, c * CW:(c + 1) * CW], start=True,
                                     stop=True).then_inc(q_done, 1)

                transpose_x(0)
                for c in range(NC):
                    if c + 1 < NC:
                        transpose_x(c + 1)
                    pe.wait_ge(xT_ready, c + 1)
                    if c == 0:
                        pe.wait_ge(w3_ready, 3)
                    if c >= 2:
                        pe.wait_ge(k_hi_ready, c - 1)
                        pe.wait_ge(k_lo_ready, c - 1)
                        pe.wait_ge(v_ready, c - 1)
                    nc.tensor.matmul(sc[1][:, c % 2, :], w3[:, 1, :], xT[:, c * CW:(c + 1) * CW], start=True,
                                     stop=True).then_inc(k_done, 1)
                    if c == 0:
                        project_q(0, pv[0][:, :])
                    for t in range(TPC):
                        last = nc.tensor.matmul(sc[2][:, c % 2, t * P:(t + 1) * P],
                                                xT[:, (c * TPC + t) * P:(c * TPC + t + 1) * P], w3[:, 2, :],
                                                start=True, stop=True)
                    last.then_inc(v_done, 1)

                def score_step(c, s):
                    g, k = divmod(s, NT)
                    first = isinstance(c, int) and c == 0
                    if k == 0:
                        pe.wait_ge(q_loaded[g], 64 * (c + 1))
                    if first and g == 0 and k % TPC == 0:
                        pe.wait_ge(k0_loaded[k // TPC], 64)
                    if first and g > 0 and k == 0:
                        pe.wait_ge(k_loaded[g], 64)
                    for half in range(2):
                        pair = 2 * s + half
                        buf = pair % PSUM_PAIRS
                        if pair >= PSUM_PAIRS:
                            user, back = pair - PSUM_PAIRS, 0
                        else:
                            user, back = next(p for p in range(2 * STEPS - 1, 0, -1) if p % PSUM_PAIRS == buf), 1
                        if not (first and back):
                            pe.wait_ge(relu[user % 2], STEPS * (c - back) + user // 2 + 1)
                        elif buf == 0:
                            pe.wait_ge(xT_ready, NC)
                        elif buf == 1:
                            pe.wait_ge(k_hi_ready, NC)
                            pe.wait_ge(k_lo_ready, NC)
                        else:
                            pe.wait_ge(v_ready, NC)
                        for i in (2 * half, 2 * half + 1):
                            rows = slice(32 * i, 32 * i + 32)
                            last = nc.tensor.matmul(sc[buf][:, i % 2, :], k_rep[rows, g, k * P:(k + 1) * P],
                                                    q_rep[rows, g, :], start=True, stop=True)
                        last.then_inc(scores[half], 1)

                def value_step(c, s):
                    g, k = divmod(s, NT)
                    first = isinstance(c, int) and c == 0
                    bank = pv[g % 2]
                    if k == 0:
                        if first:
                            pe.wait_ge(v_pad, 2 * (g + 1))
                        if not first or g >= 2:
                            pe.wait_ge(normed, G * c + g - 1)
                        if first and g == 0:
                            pe.wait_ge(q_hi_ready, 1)
                            pe.wait_ge(q_lo_ready, 1)
                        if first and g >= 2:
                            pe.wait_ge(q_lo_ready, g)
                        if not first and g == 0:
                            pe.wait_ge(q_lo_ready, NC)
                        if not first and g == 1:
                            pe.wait_ge(y_ready, c)
                        if not first and g == 2:
                            pe.wait_ge(sq_ready, 2 * c)
                    for i in range(HPG):
                        if i % 2 == 0:
                            pe.wait_ge(relu[i // 2], STEPS * c + s + 1)
                        last = nc.tensor.matmul(bank[32 * i:32 * i + 32, :], v_sb[:, k, HPG * g + i, :],
                                                w_buf[:, s % 3, i, :], start=(k == 0), stop=(k == NT - 1))
                    if k == NT - 1:
                        last.then_inc(pv_done, 1)

                def transpose_tiles(bank, src, done):
                    for t in range(TPC):
                        last = nc.tensor.transpose(bank[:, t * P:(t + 1) * P], src(t), ident[:, :])
                    last.then_inc(done, 1)

                def transpose_pv(m, bank):
                    pe.wait_ge(pv_out, m + 1)
                    transpose_tiles(bank, lambda t: pv_sb[:, t * P:(t + 1) * P], pvT_done)

                def transpose_o(j):
                    pe.wait_ge(normed, G * j + G)
                    transpose_tiles(pv[1], lambda t: o_sb[:, t, :], oT_done)

                def project_out(j):
                    pe.wait_ge(oT_ready, j + 1)
                    for t in range(TPC):
                        last = nc.tensor.matmul(pv[1][:, t * P:(t + 1) * P], oT[:, t * P:(t + 1) * P], wout_sb[:, :],
                                                start=True, stop=True)
                    last.then_inc(proj_done, 1)

                def transpose_x1(j, last_chunk=False):
                    pe.wait_ge(x1n_ready, j + 1)
                    pe.wait_ge(normed, G * j + G + (0 if last_chunk else 1))
                    transpose_tiles(pv[0], lambda t: x1n[:, t, :], x1T_done)

                def ffn(j, n, done):
                    if n == 0:
                        pe.wait_ge(x1T_ready, j + 1)
                    else:
                        pe.wait_ge(sq_ready, 2 * j + 1)
                    for t in range(TPC):
                        last = nc.tensor.matmul(pv[0][:, t * P:(t + 1) * P], x1T[:, t * P:(t + 1) * P],
                                                ffn_w[:, n, :], start=True, stop=True)
                    last.then_inc(done, 1)

                def after_pass(j, last_chunk=False):
                    return [((0, 5), lambda: transpose_o(j)), ((0, 7), lambda: project_out(j)),
                            ((1, 7), lambda: transpose_x1(j, last_chunk)), ((1, 9), lambda: ffn(j, 0, real_done)),
                            ((1, 11), lambda: ffn(j, 1, imag_done))]

                def later_queries(c):
                    pe.wait_ge(normed, c)
                    project_q(c, pv[(c + 1) % 2][:, :])

                def run_pass(c, hooks):
                    score_step(c, 0)
                    for s in range(STEPS):
                        g, k = divmod(s, NT)
                        if s + 1 < STEPS:
                            score_step(c, s + 1)
                        if k == 2 and not (isinstance(c, int) and c == 0 and g == 0):
                            transpose_pv(G * c + g - 1, pv[(g + 1) % 2])
                        for at, hook in hooks:
                            if at == (g, k):
                                hook()
                        value_step(c, s)

                run_pass(0, [((c, 7), lambda c=c: later_queries(c)) for c in range(1, NC)])
                pe.wait_ge(consts_loaded, 64)
                pe.wait_ge(ffn_w_ready, 1)
                with pe.Fori(1, NC) as c:
                    run_pass(c, after_pass(c - 1))
                transpose_pv(G * NC - 1, pv[1])
                for _, hook in after_pass(NC - 1, True):
                    hook()


_INS = ["x", "w_qkv", "w_out", "b_out", "gamma", "beta", "theta", "phi", "theta_noise", "phi_noise"]


def kernel(**inputs):
    import numpy as np
    import concourse.bacc as bacc
    from concourse.bass_utils import run_bass_kernel_spmd

    nc = bacc.Bacc("TRN2", target_bir_lowering=False, num_devices=1)
    arrays, args = {}, []
    for name in _INS:
        full = ("L0_attn_" if name in _INS[:6] else "L0_ffn_") + name
        a = np.ascontiguousarray(inputs[full])
        arrays[f"{name}_dram"] = a
        args.append(nc.dram_tensor(f"{name}_dram", a.shape, mybir.dt.from_np(a.dtype), kind="ExternalInput").ap())
    args.append(nc.dram_tensor("out_dram", (1, S, D), F32, kind="ExternalOutput").ap())
    block_kernel(nc, *args)
    r = run_bass_kernel_spmd(nc, [arrays], core_ids=[0])
    return r.results[0]["out_dram"]
```

```python
import math
from contextlib import ExitStack

import concourse.bass as bass
from concourse import mybir

F32 = mybir.dt.float32
F32R = mybir.dt.float32r
ALU = mybir.AluOpType
ACT = mybir.ActivationFunctionType

P = 128
S, D, H = 2048, 128, 16
HD = D // H
NT = S // P
TPC = 4
NC = NT // TPC
CW = TPC * P
G = 4
HPG = H // G
VW = 32
STEPS = G * NT
W_STEPS = 4
WARM_UP = 12
PSUM_PAIRS = 3
LN_EPS = 1e-5
DEN_EPS = 1e-6 * math.sqrt(HD)
TWO_PI = 2 * math.pi
ROUND = 1.5 * 2.0**23
TWO_PI_PARTS = (6.28125, 0.0019340515136718750, TWO_PI - 6.28125 - 0.0019340515136718750)
PI_BELOW = 3.1415925
NORM_SEQ = 2
POST_SEQ = 7


class Own:

    def __init__(self, engine, sem, base=0):
        self.engine, self.sem, self.base, self.n = engine, sem, base, 0

    def later(self, instruction):
        self.n += 1
        instruction.then_inc(self.sem, 1)

    def wait(self):
        self.engine.wait_ge(self.sem, self.base + self.n)

    def __call__(self, instruction):
        self.later(instruction)
        self.wait()


def block_kernel(nc, x, w_qkv, w_out, b_out, gamma, beta, theta, phi, theta_noise, phi_noise, out):
    x_v = x.rearrange("o (p t) d -> p (o t) d", p=P)
    out_v = out.rearrange("o (p t) d -> p (o t) d", p=P)
    ctx = ExitStack()
    with ctx:
        def sb(name, shape, dt=F32):
            return ctx.enter_context(nc.sbuf_tensor(name, shape, dt))

        def sem(name):
            return ctx.enter_context(nc.semaphore(name))

        ident = sb("ident", [P, P])
        x_sb = sb("x_sb", [P, NT, D])
        xn = sb("xn", [P, NT, D])
        x_beta = sb("x_beta", [P, NT, D])
        xT = sb("xT", [P, NT * P])
        wqkv_sb = sb("wqkv_sb", [P, 3 * D])
        w3 = sb("w3", [P, 3, D])
        wout_sb = sb("wout_sb", [P, D])
        bout_b = sb("bout_b", [P, D])
        gamma_b = sb("gamma_b", [P, D])
        beta_b = sb("beta_b", [P, D])
        k_hi = sb("k_hi", [P, S], F32R)
        k_lo = sb("k_lo", [P, S], F32R)
        q_hi = sb("q_hi", [P, S], F32R)
        q_lo = sb("q_lo", [P, S], F32R)
        k_rep = sb("k_rep", [P, G, S], F32R)
        q_rep = sb("q_rep", [P, G, CW], F32R)
        v_sb = sb("v_sb", [P, NT, H, VW])
        w_buf = sb("w_buf", [P, W_STEPS, HPG, CW])
        pv_sb = sb("pv_sb", [P, CW])
        den = sb("den", [P, TPC, HPG])
        o_sb = sb("o_sb", [P, TPC, D])
        oT = sb("oT", [P, CW])
        y = sb("y", [P, TPC, D])
        x1 = sb("x1", [P, TPC, D])
        x1n = sb("x1n", [P, TPC, D])
        x1T = sb("x1T", [P, CW])
        sq = sb("sq", [P, TPC, 2, D])
        mag = sb("mag", [P, TPC, D])
        x2 = sb("x2", [P, TPC, D])
        angles = sb("angles", [P, 4, D])
        turns = sb("turns", [P, 2, D])
        ffn_w = sb("ffn_w", [P, 2, D])
        stats = sb("stats", [P, NT, 6])
        mv = sb("mv", [P, NT, 2])
        inv_var = sb("inv_var", [P, NT])
        rstd = sb("rstd", [P, NT])
        stats_p = sb("stats_p", [P, TPC, 6])
        mv_p = sb("mv_p", [P, TPC, 2])
        iv_p = sb("iv_p", [P, 2, TPC])
        spare = sb("spare", [P, 1])
        spare_act = sb("spare_act", [P, 1])
        rs_p = sb("rs_p", [P, 2, TPC])

        sc = [ctx.enter_context(nc.psum_tensor(f"sc{i}", [P, 2, CW], F32)) for i in range(PSUM_PAIRS)]
        pv = [ctx.enter_context(nc.psum_tensor(f"pv{i}", [P, CW], F32)) for i in range(2)]

        xT_bank = [sc[0][:, 0, :], sc[0][:, 1, :], pv[1][:, :], pv[1][:, :]]
        k_bank = [sc[1][:, 0, :], sc[1][:, 1, :], pv[1][:, :], pv[1][:, :]]
        v_bank = [sc[2][:, 0, :], pv[0][:, :], pv[1][:, :], pv[1][:, :]]
        q_bank = [pv[0][:, :], pv[0][:, :], pv[1][:, :], pv[0][:, :]]

        x_loaded = [sem(f"x_loaded{c}") for c in range(NC)]
        wqkv_loaded = sem("wqkv_loaded")
        consts_loaded = sem("consts_loaded")
        angles_loaded = sem("angles_loaded")
        ident_zero = sem("ident_zero")
        ident_ready = sem("ident_ready")
        w3_ready = sem("w3_ready")
        v_pad = sem("v_pad")
        ln_own = sem("ln_own")
        var_ready = sem("var_ready")
        rstd_ready = sem("rstd_ready")
        xn_ready = sem("xn_ready")
        xT_done = sem("xT_done")
        xT_ready = sem("xT_ready")
        k_done = sem("k_done")
        q_done = sem("q_done")
        v_done = sem("v_done")
        k_hi_ready = sem("k_hi_ready")
        k_lo_ready = sem("k_lo_ready")
        q_hi_ready = sem("q_hi_ready")
        q_lo_ready = sem("q_lo_ready")
        v_ready = sem("v_ready")
        k0_loaded = [sem(f"k0_loaded{c}") for c in range(NC)]
        k_loaded = [None] + [sem(f"k_loaded{g}") for g in range(1, G)]
        q_first = sem("q_first")
        q_loaded = [sem(f"q_loaded{g}") for g in range(G)]
        xb_ready = sem("xb_ready")
        trig_own = sem("trig_own")
        angles_ready = sem("angles_ready")
        ffn_w_ready = sem("ffn_w_ready")
        scores = [sem("scores_act"), sem("scores_dve")]
        relu = [sem("relu_act"), sem("relu_dve")]
        pv_done = sem("pv_done")
        pv_out = sem("pv_out")
        pvT_done = sem("pvT_done")
        norm_own = sem("norm_own")
        normed = sem("normed")
        oT_done = sem("oT_done")
        oT_ready = sem("oT_ready")
        proj_done = sem("proj_done")
        y_ready = sem("y_ready")
        post_own = [sem("post_own0"), sem("post_own1")]
        iv_ready = [sem("iv_ready0"), sem("iv_ready1")]
        rs_ready = [sem("rs_ready0"), sem("rs_ready1")]
        x1_ready = sem("x1_ready")
        x1n_ready = sem("x1n_ready")
        x1T_done = sem("x1T_done")
        x1T_ready = sem("x1T_ready")
        ffn_done = sem("ffn_done")
        sq_ready = sem("sq_ready")
        sum_ready = sem("sum_ready")
        mag_ready = sem("mag_ready")
        x2_ready = sem("x2_ready")
        stored = sem("stored")

        def chunk(c):
            return bass.ds(c * TPC, TPC)

        class Part:

            def __init__(self, j, half=None):
                self.j, self.half = j, half
                self.n = j if half is None else j + half
                self.lo, self.tiles = (0, TPC) if half is None else (2 * half, 2)
                self.own = (post_own[half or 0], POST_SEQ * (0 if half else j))
                if half is None:
                    self.o_bank = self.y_bank = pv[1]
                    self.x1_bank = self.ffn_bank = pv[0]
                else:
                    self.pv_bank, self.o_bank = sc[half][:, 0, :], sc[half][:, 1, :]
                    self.y_bank = sc[2][:, half, :]
                    self.x1_bank, self.ffn_bank = self.pv_bank, self.o_bank

            def sl(self):
                return slice(self.lo, self.lo + self.tiles)

            def cols(self):
                return slice(self.lo * P, (self.lo + self.tiles) * P)

            def all(self):
                return range(self.lo, self.lo + self.tiles)

            def rows(self):
                return bass.ds(self.j * TPC + self.lo, self.tiles)

            def pairs(self):
                if self.half is None:
                    return [(2 * self.j, 0), (2 * self.j + 1, 2)]
                return [(2 * self.j + self.half, self.lo)]

        def row(v, d):
            return v[:, :].unsqueeze(1).to_broadcast([P, d, D])

        with nc.Block() as block:
            @block.sync
            def _(sp):
                def replicate_q(c, g):
                    for j in range(4):
                        src = q_lo if j % 2 else q_hi
                        sp.dma_start(
                            q_rep[j:P:4, g, :].bitcast(F32),
                            src[32 * g:32 * g + 32, bass.ds(c * CW, CW)].bitcast(F32),
                        ).then_inc(q_loaded[g], 16)

                def replicate_k(g, lo, n, done, parts=range(4)):
                    for j in parts:
                        src = k_lo if j // 2 else k_hi
                        sp.dma_start(
                            k_rep[j:P:4, g, lo:lo + n].bitcast(F32),
                            src[32 * g:32 * g + 32, lo:lo + n].bitcast(F32),
                        ).then_inc(done, 16)

                def store(part):
                    sp.wait_ge(x2_ready, part.n + 1)
                    sp.dma_start(out_v[:, part.rows(), :], x2[:, part.sl(), :]).then_inc(stored, 16)

                def next_queries(c, g):
                    if isinstance(c, int):
                        sp.wait_ge(q_lo_ready, c + 2)
                    for s in scores:
                        sp.wait_ge(s, STEPS * c + NT * (g + 1))
                    replicate_q(c + 1, g)

                sp.dma_start(x_sb[:, 0:TPC, :], x_v[:, 0:TPC, :]).then_inc(x_loaded[0], 16)
                sp.dma_start(wqkv_sb[:, :], w_qkv).then_inc(wqkv_loaded, 16)
                for c in range(1, NC):
                    sp.dma_start(x_sb[:, chunk(c), :], x_v[:, chunk(c), :]).then_inc(x_loaded[c], 16)
                for dst, src in ((bout_b, b_out), (gamma_b, gamma), (beta_b, beta)):
                    sp.dma_start(dst[:, :], src.partition_broadcast(P)).then_inc(consts_loaded, 16)
                sp.dma_start(wout_sb[:, :], w_out).then_inc(consts_loaded, 16)
                for n, src in enumerate((theta, phi, theta_noise, phi_noise)):
                    sp.dma_start(angles[:, n, :], src).then_inc(angles_loaded, 16)
                for c in range(NC):
                    sp.wait_ge(k_hi_ready, c + 1)
                    replicate_k(0, c * CW, CW, k0_loaded[c], (0, 1))
                    sp.wait_ge(k_lo_ready, c + 1)
                    replicate_k(0, c * CW, CW, k0_loaded[c], (2, 3))
                    if c == 0:
                        sp.wait_ge(q_lo_ready, 1)
                        for j in (1, 3):
                            sp.dma_start(q_rep[j:P:4, 0, :].bitcast(F32),
                                         q_lo[0:32, 0:CW].bitcast(F32)).then_inc(q_loaded[0], 16)
                for g in range(1, G):
                    replicate_q(0, g)
                    replicate_k(g, 0, S, k_loaded[g])

                for g in range(G):
                    next_queries(0, g)
                with sp.Fori(1, NC - 1) as c:
                    next_queries(c, 0)
                    next_queries(c, 1)
                    store(Part(c - 1))
                    next_queries(c, 2)
                    next_queries(c, 3)
                store(Part(NC - 2))
                store(Part(NC - 1, 0))
                store(Part(NC - 1, 1))
                sp.wait_ge(stored, 16 * (NC + 1))

            @block.gpsimd
            def _(pool):
                nc.gpsimd.memset(ident[:, :], 0.0).then_inc(ident_zero, 1)
                pool.wait_ge(ident_zero, 1)
                nc.gpsimd.affine_select(out=ident[:, :], in_=ident[:, :], compare_op=ALU.not_equal, fill=1.0,
                                        base=0, pattern=[[-1, P]], channel_multiplier=1).then_inc(ident_ready, 1)
                pool.wait_ge(wqkv_loaded, 16)
                for n in range(3):
                    src = wqkv_sb[:, :].rearrange("p (h c d) -> p c h d", h=H, c=3)[:, n]
                    nc.gpsimd.tensor_copy(w3[:, n, :].rearrange("p (h d) -> p h d", h=H), src).then_inc(w3_ready, 1)
                for g in range(G):
                    heads = slice(HPG * g, HPG * (g + 1))
                    nc.gpsimd.memset(v_sb[:, :, heads, HD + 1:VW], 0.0).then_inc(v_pad, 1)
                    nc.gpsimd.memset(v_sb[:, :, heads, HD:HD + 1], 1.0).then_inc(v_pad, 1)
                    if g == 0:
                        pool.wait_ge(q_hi_ready, 1)
                        for j in (0, 2):
                            pool.dma_start(q_rep[j:P:4, 0, :].bitcast(F32),
                                           q_hi[0:32, 0:CW].bitcast(F32)).then_inc(q_first, 16)
                pool.wait_ge(consts_loaded, 64)
                pool.wait_ge(xn_ready, NC)
                pool.wait_ge(xT_done, NC)
                for c in range(NC):
                    nc.gpsimd.tensor_tensor(xn[:, chunk(c), :], xn[:, chunk(c), :], row(bout_b, TPC),
                                            ALU.add).then_inc(xb_ready, 1)
                    nc.gpsimd.tensor_tensor(x_beta[:, chunk(c), :], x_sb[:, chunk(c), :], row(beta_b, TPC),
                                            ALU.add).then_inc(xb_ready, 1)

                def finish(part):
                    for n, t in part.pairs():
                        pool.wait_ge(sq_ready, n + 1)
                        nc.gpsimd.tensor_tensor(mag[:, t:t + 2, :], sq[:, t:t + 2, 0, :], sq[:, t:t + 2, 1, :],
                                                ALU.add).then_inc(sum_ready, 1)
                    pool.wait_ge(mag_ready, part.n + 1)
                    nc.gpsimd.tensor_tensor(x2[:, :, :], mag[:, :, :], x1[:, :, :], ALU.add).then_inc(x2_ready, 1)

                finish(Part(0))
                with pool.Fori(1, NC - 1) as c:
                    pool.wait_ge(x2_ready, c)
                    pool.wait_ge(stored, 16 * c)
                    finish(Part(c))

            @block.scalar
            def _(act):
                def root(c):
                    act.wait_ge(var_ready, c + 1)
                    nc.scalar.activation(rstd[:, chunk(c)], inv_var[:, chunk(c)], ACT.Sqrt).then_inc(rstd_ready, 1)

                def take_xT(c):
                    act.wait_ge(xT_done, c + 1)
                    nc.scalar.copy(xT[:, c * CW:(c + 1) * CW], xT_bank[c]).then_inc(xT_ready, 1)

                def take_k(c):
                    act.wait_ge(k_done, c + 1)
                    nc.scalar.copy(k_hi[:, c * CW:(c + 1) * CW], k_bank[c]).then_inc(k_hi_ready, 1)

                def take_q(c):
                    act.wait_ge(q_done, c + 1)
                    nc.scalar.copy(q_hi[:, c * CW:(c + 1) * CW], q_bank[c]).then_inc(q_hi_ready, 1)

                def take_v(c):
                    act.wait_ge(v_done, c + 1)
                    nc.scalar.copy(v_sb[:, chunk(c), :, 0:HD],
                                   v_bank[c].rearrange("p (t h d) -> p t h d", t=TPC, h=H)).then_inc(v_ready, 1)

                root(0)
                root(1)
                take_xT(0)
                take_k(0)
                take_q(0)
                root(2)
                take_xT(1)
                take_v(0)
                take_k(1)
                root(3)
                take_xT(2)

                def relu_step(c, s):
                    act.wait_ge(scores[0], STEPS * c + s + 1)
                    nc.scalar.activation(w_buf[:, s % W_STEPS, 0:2, :], sc[2 * s % PSUM_PAIRS][:, :, :],
                                         ACT.Relu).then_inc(relu[0], 1)

                def take_pv(m, bank):
                    act.wait_ge(pv_done, m + 1)
                    if not isinstance(m, int) or m > 0:
                        act.wait_ge(pvT_done, m)
                    nc.scalar.copy(pv_sb[:, :], bank[:, :]).then_inc(pv_out, 1)

                def trig():
                    act.wait_ge(angles_ready, 1)
                    nc.scalar.activation(ffn_w[:, :, :], angles[:, 0:2, :], ACT.Sin).then_inc(ffn_w_ready, 1)

                def sqrt_table():
                    nc.scalar.activation(spare_act[:, :], rstd[:, 0:1], ACT.Sqrt)

                def take_oT(part):
                    act.wait_ge(oT_done, part.n + 1)
                    nc.scalar.copy(oT[:, part.cols()], part.o_bank[:, 0:part.tiles * P]).then_inc(oT_ready, 1)

                def post_root(part, norm):
                    act.wait_ge(iv_ready[norm], part.n + 1)
                    nc.scalar.activation(rs_p[:, norm, part.sl()], iv_p[:, norm, part.sl()],
                                         ACT.Sqrt).then_inc(rs_ready[norm], 1)

                def take_x1T(part):
                    act.wait_ge(x1T_done, part.n + 1)
                    nc.scalar.copy(x1T[:, part.cols()], part.x1_bank[:, 0:part.tiles * P]).then_inc(x1T_ready, 1)

                def square(part, pair):
                    n, t = part.pairs()[pair]
                    act.wait_ge(ffn_done, n + 1)
                    nc.scalar.activation(sq[:, t:t + 2, :, :].rearrange("p t c d -> p (t c d)"),
                                         part.ffn_bank[:, :], ACT.Square).then_inc(sq_ready, 1)

                def magnitude(part):
                    act.wait_ge(sum_ready, part.pairs()[-1][0] + 1)
                    nc.scalar.activation(mag[:, part.sl(), :], mag[:, part.sl(), :], ACT.Sqrt).then_inc(mag_ready, 1)

                def after_pass(j):
                    part = Part(j)
                    return [((0, 6), lambda: take_oT(part)), ((0, 12), lambda: post_root(part, 0)),
                            ((1, 3), lambda: post_root(part, 1)), ((1, 8), lambda: take_x1T(part)),
                            ((1, 10), lambda: square(part, 0)), ((1, 12), lambda: square(part, 1)),
                            ((1, 14), lambda: magnitude(part))]

                def run_pass(c, hooks):
                    for g in range(G):
                        for k in range(NT):
                            relu_step(c, NT * g + k)
                            if k == 1 and not (isinstance(c, int) and c == 0 and g == 0):
                                take_pv(G * c + g - 1, pv[(g + 1) % 2])
                            for at, hook in hooks:
                                if at == (g, k):
                                    hook()

                run_pass(0, [((0, 0), lambda: take_v(1)), ((0, 1), lambda: take_xT(3)), ((0, 3), lambda: take_k(2)), ((0, 5), lambda: take_k(3)),
                             ((0, 7), lambda: take_v(2)), ((0, 9), lambda: take_v(3)),
                             ((1, 8), lambda: take_q(1)), ((2, 8), lambda: take_q(2)),
                             ((3, 8), lambda: take_q(3)), ((2, 12), trig), ((3, 3), sqrt_table)])
                with act.Fori(1, NC) as c:
                    run_pass(c, after_pass(c - 1))
                halves = [Part(NC - 1, 0), Part(NC - 1, 1)]
                act.wait_ge(pv_done, G * NC)
                act.wait_ge(pvT_done, G * NC - 1)
                for part in halves:
                    nc.scalar.copy(pv_sb[:, part.cols()], pv[1][:, part.cols()]).then_inc(pv_out, 1)
                for stage in (take_oT, lambda p: post_root(p, 0), lambda p: post_root(p, 1), take_x1T,
                              lambda p: square(p, 0), magnitude):
                    for part in halves:
                        stage(part)

            @block.vector
            def _(dve):
                own = Own(dve, ln_own)

                def statistics(c):
                    dve.wait_ge(x_loaded[c], 16)
                    for t in range(c * TPC, (c + 1) * TPC):
                        last = nc.vector.bn_stats(stats[:, t, :], x_sb[:, t, :])
                    own(last)
                    for t in range(c * TPC, (c + 1) * TPC):
                        last = nc.vector.bn_aggr(mv[:, t, :], stats[:, t, :])
                    own(last)
                    own(nc.vector.tensor_scalar_add(inv_var[:, chunk(c)], mv[:, chunk(c), 1], LN_EPS))
                    nc.vector.reciprocal(inv_var[:, chunk(c)], inv_var[:, chunk(c)]).then_inc(var_ready, 1)

                def normalise_x(c):
                    dve.wait_ge(rstd_ready, c + 1)
                    for t in range(c * TPC, (c + 1) * TPC):
                        last = nc.vector.tensor_scalar(xn[:, t, :], x_sb[:, t, :], mv[:, t, 0:1], rstd[:, t:t + 1],
                                                       ALU.subtract, ALU.mult)
                    last.then_inc(xn_ready, 1)

                def low_part(lo, hi, hi_ready, lo_ready, c, bank):
                    cols = slice(c * CW, (c + 1) * CW)
                    dve.wait_ge(hi_ready, c + 1)
                    nc.vector.tensor_tensor(lo[:, cols], bank, hi[:, cols].bitcast(F32),
                                            ALU.subtract).then_inc(lo_ready, 1)

                def take_k(c):
                    low_part(k_lo, k_hi, k_hi_ready, k_lo_ready, c, k_bank[c])

                def take_q(c):
                    low_part(q_lo, q_hi, q_hi_ready, q_lo_ready, c, q_bank[c])

                statistics(0)
                normalise_x(0)
                statistics(1)
                normalise_x(1)
                statistics(2)
                take_k(0)
                take_q(0)
                normalise_x(2)
                take_k(1)
                statistics(3)
                normalise_x(3)

                def relu_step(c, s):
                    dve.wait_ge(scores[1], STEPS * c + s + 1)
                    nc.vector.tensor_scalar(w_buf[:, s % W_STEPS, 2:4, :], sc[(2 * s + 1) % PSUM_PAIRS][:, :, :],
                                            0.0, None, ALU.max).then_inc(relu[1], 1)

                def normalise(m, bank, g, tiles=slice(0, TPC), c=None):
                    own = Own(dve, norm_own, NORM_SEQ * m)
                    n = tiles.stop - tiles.start
                    pvT = bank[:, 0:n * P].rearrange("p (t i v) -> p t i v", t=n, i=HPG)
                    dve.wait_ge(pvT_done, m + 1)
                    own(nc.vector.tensor_scalar_add(den[:, tiles, :], pvT[:, :, :, HD], DEN_EPS))
                    own(nc.vector.reciprocal(den[:, tiles, :], den[:, tiles, :]))
                    if g == 0 and not isinstance(c, int):
                        dve.wait_ge(oT_done, c)
                    nc.vector.tensor_tensor(
                        o_sb[:, tiles, 32 * g:32 * g + 32].rearrange("p t (i d) -> p t i d", i=HPG),
                        pvT[:, :, :, 0:HD], den[:, tiles, :].unsqueeze(3).to_broadcast([P, n, HPG, HD]),
                        ALU.mult).then_inc(normed, 1)

                def trig_angles(own):
                    both = angles[:, 0:2, :]

                    def add_noise():
                        dve.wait_ge(angles_loaded, 64)
                        own(nc.vector.tensor_tensor(both, both, angles[:, 2:4, :], ALU.add))

                    def in_turns():
                        nc.vector.tensor_scalar(turns[:, 0, :], angles[:, 0, :], 1 / TWO_PI, 0.25, ALU.mult, ALU.add)
                        own(nc.vector.tensor_scalar(turns[:, 1, :], angles[:, 1, :], 1 / TWO_PI, None, ALU.mult))

                    def whole_turns():
                        own(nc.vector.tensor_scalar_add(turns[:, :, :], turns[:, :, :], ROUND))
                        own(nc.vector.tensor_scalar_add(turns[:, :, :], turns[:, :, :], -ROUND))

                    def subtract(part):
                        own(nc.vector.scalar_tensor_tensor(out=both, in0=turns[:, :, :], scalar=-part, in1=both,
                                                           op0=ALU.mult, op1=ALU.add))

                    def clamp():
                        own(nc.vector.tensor_scalar_add(angles[:, 0, :], angles[:, 0, :], math.pi / 2))
                        nc.vector.tensor_scalar(both, both, PI_BELOW, -PI_BELOW, ALU.min,
                                                ALU.max).then_inc(angles_ready, 1)

                    return [add_noise, in_turns, whole_turns,
                            *(lambda part=part: subtract(part) for part in TWO_PI_PARTS), clamp]

                def residual(part):
                    dve.wait_ge(proj_done, part.n + 1)
                    nc.vector.tensor_tensor(
                        y[:, part.sl(), :],
                        part.y_bank[:, 0:part.tiles * P].rearrange("p (t d) -> p t d", t=part.tiles),
                        xn[:, part.rows(), :], ALU.add).then_inc(y_ready, 1)
                    dve.wait_ge(y_ready, part.n + 1)

                def post_stats(part, src):
                    for t in part.all():
                        last = nc.vector.bn_stats(stats_p[:, t, :], src[:, t, :])
                    part.chain(last)

                def post_inverse(part, norm):
                    nc.vector.memset(spare[:, :], 0.0)
                    for t in part.all():
                        last = nc.vector.bn_aggr(mv_p[:, t, :], stats_p[:, t, :])
                    part.chain(last)
                    part.chain(nc.vector.tensor_scalar_add(iv_p[:, norm, part.sl()], mv_p[:, part.sl(), 1], LN_EPS))
                    nc.vector.reciprocal(iv_p[:, norm, part.sl()],
                                         iv_p[:, norm, part.sl()]).then_inc(iv_ready[norm], 1)

                def times_gamma(part):
                    for t in part.all():
                        last = nc.vector.scalar_tensor_tensor(out=y[:, t, :], in0=y[:, t, :], scalar=mv_p[:, t, 0:1],
                                                              in1=gamma_b[:, :], op0=ALU.subtract, op1=ALU.mult)
                    part.chain.later(last)

                def first_residual(part):
                    dve.wait_ge(rs_ready[0], part.n + 1)
                    part.chain.wait()
                    for t in part.all():
                        last = nc.vector.scalar_tensor_tensor(
                            out=x1[:, t, :], in0=y[:, t, :], scalar=rs_p[:, 0, t:t + 1],
                            in1=x_beta[:, bass.ds(part.j * TPC + t, 1), :].rearrange("p o d -> p (o d)"),
                            op0=ALU.mult, op1=ALU.add)
                    last.then_inc(x1_ready, 1)
                    dve.wait_ge(x1_ready, part.n + 1)

                def normalise_x1(part):
                    dve.wait_ge(rs_ready[1], part.n + 1)
                    for t in part.all():
                        last = nc.vector.tensor_scalar(x1n[:, t, :], x1[:, t, :], mv_p[:, t, 0:1],
                                                       rs_p[:, 1, t:t + 1], ALU.subtract, ALU.mult)
                    last.then_inc(x1n_ready, 1)

                def start_chain(part):
                    part.chain = Own(dve, *part.own)
                    return part

                def after_pass(j):
                    part = start_chain(Part(j))
                    return [((0, 8), lambda: residual(part)), ((0, 9), lambda: post_stats(part, y)),
                            ((0, 10), lambda: post_inverse(part, 0)), ((0, 11), lambda: times_gamma(part)),
                            ((0, 13), lambda: first_residual(part)), ((0, 14), lambda: post_stats(part, x1)),
                            ((1, 1), lambda: post_inverse(part, 1)), ((1, 5), lambda: normalise_x1(part)),
                            ((3, 0), lambda: dve.wait_ge(x2_ready, part.n + 1))]

                def run_pass(c, hooks):
                    for g in range(G):
                        for k in range(NT):
                            relu_step(c, NT * g + k)
                            if k == 3 and not (isinstance(c, int) and c == 0 and g == 0):
                                normalise(G * c + g - 1, pv[(g + 1) % 2], (g - 1) % G, c=c)
                            for at, hook in hooks:
                                if at == (g, k):
                                    hook()

                own = Own(dve, trig_own)
                run_pass(0, [((0, 3), lambda: take_k(2)), ((0, 5), lambda: take_k(3)),
                             ((1, 8), lambda: take_q(1)), ((2, 8), lambda: take_q(2)),
                             ((3, 8), lambda: take_q(3))]
                         + [((1 + n // 8, 9 + n % 8 if n < 7 else n - 7), part)
                            for n, part in enumerate(trig_angles(own))])
                dve.wait_ge(xb_ready, 2 * NC)
                dve.wait_ge(consts_loaded, 64)
                with dve.Fori(1, NC) as c:
                    run_pass(c, after_pass(c - 1))
                halves = [start_chain(Part(NC - 1, 0)), start_chain(Part(NC - 1, 1))]

                def tail_sum(part):
                    dve.wait_ge(sq_ready, part.pairs()[0][0] + 1)
                    nc.vector.tensor_tensor(mag[:, part.sl(), :], sq[:, part.sl(), 0, :], sq[:, part.sl(), 1, :],
                                            ALU.add).then_inc(sum_ready, 1)

                def tail_finish(part):
                    dve.wait_ge(mag_ready, part.n + 1)
                    nc.vector.tensor_tensor(x2[:, part.sl(), :], mag[:, part.sl(), :], x1[:, part.sl(), :],
                                            ALU.add).then_inc(x2_ready, 1)

                for part in halves:
                    normalise(G * NC - 1 + part.half, part.pv_bank, G - 1, part.sl())
                for stage in (residual, lambda p: post_stats(p, y), lambda p: post_inverse(p, 0), times_gamma,
                              first_residual, lambda p: post_stats(p, x1), lambda p: post_inverse(p, 1),
                              normalise_x1):
                    for part in halves:
                        stage(part)
                dve.wait_ge(x2_ready, NC - 1)
                dve.wait_ge(stored, 16 * (NC - 1))
                for stage in (tail_sum, tail_finish):
                    for part in halves:
                        stage(part)

            @block.tensor
            def _(pe):
                def transpose_x(c):
                    pe.wait_ge(xn_ready, c + 1)
                    if c == 3:
                        pe.wait_ge(xT_ready, 3)
                    for t in range(TPC):
                        last = nc.tensor.transpose(xT_bank[c][:, t * P:(t + 1) * P], xn[:, c * TPC + t, :],
                                                   ident[:, :])
                    last.then_inc(xT_done, 1)

                def project_k(c):
                    if c == 2:
                        pe.wait_ge(xT_ready, 4)
                    elif c == 3:
                        pe.wait_ge(k_hi_ready, 3)
                        pe.wait_ge(k_lo_ready, 3)
                    else:
                        pe.wait_ge(xT_ready, c + 1)
                    nc.tensor.matmul(k_bank[c], w3[:, 1, :], xT[:, c * CW:(c + 1) * CW], start=True,
                                     stop=True).then_inc(k_done, 1)

                def project_q(c):
                    if c > 0:
                        pe.wait_ge(normed, c)
                    nc.tensor.matmul(q_bank[c], w3[:, 0, :], xT[:, c * CW:(c + 1) * CW], start=True,
                                     stop=True).then_inc(q_done, 1)

                def project_v(c):
                    if c == 2:
                        pe.wait_ge(k_hi_ready, 4)
                        pe.wait_ge(k_lo_ready, 4)
                    elif c == 3:
                        pe.wait_ge(v_ready, 3)
                    for t in range(TPC):
                        last = nc.tensor.matmul(v_bank[c][:, t * P:(t + 1) * P],
                                                xT[:, (c * TPC + t) * P:(c * TPC + t + 1) * P], w3[:, 2, :],
                                                start=True, stop=True)
                    last.then_inc(v_done, 1)

                def warm_up(n):
                    for _ in range(n):
                        nc.tensor.matmul(pv[0][:, 0:P], ident[:, :], ident[:, :], start=True, stop=True)

                pe.wait_ge(ident_ready, 1)
                warm_up(WARM_UP)
                transpose_x(0)
                pe.wait_ge(w3_ready, 3)
                project_k(0)
                project_q(0)
                transpose_x(1)
                project_k(1)
                project_v(0)
                transpose_x(2)
                pe.wait_ge(q_lo_ready, 1)
                warm_up(WARM_UP // 2)

                def score_step(c, s):
                    g, k = divmod(s, NT)
                    first = isinstance(c, int) and c == 0
                    if k == 0:
                        if first and g == 0:
                            pe.wait_ge(q_first, 32)
                            pe.wait_ge(q_loaded[0], 32)
                        else:
                            pe.wait_ge(q_loaded[g], 64 * (c + 1) - (32 if g == 0 else 0))
                    if first and g == 0 and k % TPC == 0:
                        pe.wait_ge(k0_loaded[k // TPC], 64)
                    if first and g > 0 and k == 0:
                        pe.wait_ge(k_loaded[g], 64)
                    for half in range(2):
                        pair = 2 * s + half
                        buf = pair % PSUM_PAIRS
                        if pair >= PSUM_PAIRS:
                            user, back = pair - PSUM_PAIRS, 0
                        else:
                            user, back = next(p for p in range(2 * STEPS - 1, 0, -1) if p % PSUM_PAIRS == buf), 1
                        if not (first and back):
                            pe.wait_ge(relu[user % 2], STEPS * (c - back) + user // 2 + 1)
                        elif buf == 0:
                            pe.wait_ge(xT_ready, 2)
                        elif buf == 1:
                            pe.wait_ge(k_hi_ready, 2)
                            pe.wait_ge(k_lo_ready, 2)
                        else:
                            pe.wait_ge(v_ready, 1)
                        for i in (2 * half, 2 * half + 1):
                            rows = slice(32 * i, 32 * i + 32)
                            last = nc.tensor.matmul(sc[buf][:, i % 2, :], k_rep[rows, g, k * P:(k + 1) * P],
                                                    q_rep[rows, g, :], start=True, stop=True)
                        last.then_inc(scores[half], 1)

                def value_step(c, s):
                    g, k = divmod(s, NT)
                    first = isinstance(c, int) and c == 0
                    bank = pv[g % 2]
                    if k == 0:
                        if first:
                            pe.wait_ge(v_pad, 2 * (g + 1))
                        if not first or g >= 2:
                            pe.wait_ge(normed, G * c + g - 1)
                        if first and g == 1:
                            pe.wait_ge(v_ready, NC)
                        if first and g >= 2:
                            pe.wait_ge(q_lo_ready, g)
                        if not first and g == 0:
                            pe.wait_ge(q_lo_ready, NC)
                        if not first and g == 1:
                            pe.wait_ge(y_ready, c)
                        if not first and g == 2:
                            pe.wait_ge(sq_ready, 2 * c)
                    if first and g == 0 and k % TPC == 0:
                        pe.wait_ge(v_ready, max(2, k // TPC + 1))
                    for i in (1, 2, 3, 0):
                        if i in (1, 2):
                            pe.wait_ge(relu[i // 2], STEPS * c + s + 1)
                        last = nc.tensor.matmul(bank[32 * i:32 * i + 32, :], v_sb[:, k, HPG * g + i, :],
                                                w_buf[:, s % W_STEPS, i, :], start=(k == 0), stop=(k == NT - 1))
                    if k == NT - 1:
                        last.then_inc(pv_done, 1)

                def transpose_tiles(bank, src, tiles, done):
                    for n, t in enumerate(tiles):
                        last = nc.tensor.transpose(bank[:, n * P:(n + 1) * P], src(t), ident[:, :])
                    last.then_inc(done, 1)

                def transpose_pv(m, bank, tiles=range(TPC)):
                    pe.wait_ge(pv_out, m + 1)
                    transpose_tiles(bank, lambda t: pv_sb[:, t * P:(t + 1) * P], tiles, pvT_done)

                def transpose_o(part):
                    pe.wait_ge(normed, G * part.j + G + (part.half or 0))
                    transpose_tiles(part.o_bank, lambda t: o_sb[:, t, :], part.all(), oT_done)

                def project_out(part):
                    pe.wait_ge(oT_ready, part.n + 1)
                    for n, t in enumerate(part.all()):
                        last = nc.tensor.matmul(part.y_bank[:, n * P:(n + 1) * P], oT[:, t * P:(t + 1) * P],
                                                wout_sb[:, :], start=True, stop=True)
                    last.then_inc(proj_done, 1)

                def transpose_x1(part):
                    pe.wait_ge(x1n_ready, part.n + 1)
                    if part.half is None:
                        pe.wait_ge(normed, G * part.j + G + 1)
                    transpose_tiles(part.x1_bank, lambda t: x1n[:, t, :], part.all(), x1T_done)

                def ffn(part, pair):
                    n, t = part.pairs()[pair]
                    if pair == 0:
                        pe.wait_ge(x1T_ready, part.n + 1)
                    else:
                        pe.wait_ge(sq_ready, n)
                    for i in range(2):
                        last = nc.tensor.matmul(part.ffn_bank[:, i * 2 * D:(i + 1) * 2 * D],
                                                x1T[:, (t + i) * P:(t + i + 1) * P],
                                                ffn_w[:, :, :].rearrange("p c d -> p (c d)"), start=True, stop=True)
                    last.then_inc(ffn_done, 1)

                def after_pass(j):
                    part = Part(j)
                    return [((0, 5), lambda: transpose_o(part)), ((0, 7), lambda: project_out(part)),
                            ((1, 7), lambda: transpose_x1(part)), ((1, 9), lambda: ffn(part, 0)),
                            ((1, 11), lambda: ffn(part, 1))]

                def run_pass(c, hooks):
                    for s in range(STEPS):
                        score_step(c, s)
                        if s == 0:
                            if isinstance(c, int) and c == 0:
                                project_v(1)
                            else:
                                value_step(c - 1, STEPS - 1)
                            continue
                        g, k = divmod(s - 1, NT)
                        if k == 2 and not (isinstance(c, int) and c == 0 and g == 0):
                            transpose_pv(G * c + g - 1, pv[(g + 1) % 2])
                        for at, hook in hooks:
                            if at == (g, k):
                                hook()
                        value_step(c, s - 1)

                run_pass(0, [((0, 0), lambda: transpose_x(3)), ((0, 2), lambda: project_k(2)),
                             ((0, 4), lambda: project_k(3)), ((0, 6), lambda: project_v(2)),
                             ((0, 8), lambda: project_v(3))]
                         + [((c, 7), lambda c=c: project_q(c)) for c in range(1, NC)])
                pe.wait_ge(consts_loaded, 64)
                pe.wait_ge(ffn_w_ready, 1)
                with pe.Fori(1, NC) as c:
                    run_pass(c, after_pass(c - 1))
                value_step(NC - 1, STEPS - 1)
                halves = [Part(NC - 1, 0), Part(NC - 1, 1)]
                for part in halves:
                    transpose_pv(G * NC - 1 + part.half, part.pv_bank, part.all())
                for stage in (transpose_o, project_out, transpose_x1, lambda p: ffn(p, 0)):
                    for part in halves:
                        stage(part)


_INS = ["x", "w_qkv", "w_out", "b_out", "gamma", "beta", "theta", "phi", "theta_noise", "phi_noise"]


def kernel(**inputs):
    import numpy as np
    import concourse.bacc as bacc
    from concourse.bass_utils import run_bass_kernel_spmd

    nc = bacc.Bacc("TRN2", target_bir_lowering=False, num_devices=1)
    arrays, args = {}, []
    for name in _INS:
        full = ("L0_attn_" if name in _INS[:6] else "L0_ffn_") + name
        a = np.ascontiguousarray(inputs[full])
        arrays[f"{name}_dram"] = a
        args.append(nc.dram_tensor(f"{name}_dram", a.shape, mybir.dt.from_np(a.dtype), kind="ExternalInput").ap())
    args.append(nc.dram_tensor("out_dram", (1, S, D), F32, kind="ExternalOutput").ap())
    block_kernel(nc, *args)
    r = run_bass_kernel_spmd(nc, [arrays], core_ids=[0])
    return r.results[0]["out_dram"]
```

```python
import math
from contextlib import ExitStack

import concourse.bass as bass
from concourse import mybir

F32 = mybir.dt.float32
F32R = mybir.dt.float32r
ALU = mybir.AluOpType
ACT = mybir.ActivationFunctionType

P = 128
S, D, H = 2048, 128, 16
HD = D // H
NT = S // P
TPC = 4
NC = NT // TPC
CW = TPC * P
G = 4
HPG = H // G
VW = 32
STEPS = G * NT
W_STEPS = 4
WARM_UP = 12
TAIL_WARM_UP = 20
PSUM_PAIRS = 3
LN_EPS = 1e-5
DEN_EPS = 1e-6 * math.sqrt(HD)
TWO_PI = 2 * math.pi
ROUND = 1.5 * 2.0**23
TWO_PI_PARTS = (6.28125, 0.0019340515136718750, TWO_PI - 6.28125 - 0.0019340515136718750)
PI_BELOW = 3.1415925
NORM_SEQ = 2
POST_SEQ = 7


class Own:

    def __init__(self, engine, sem, base=0):
        self.engine, self.sem, self.base, self.n = engine, sem, base, 0

    def later(self, instruction):
        self.n += 1
        instruction.then_inc(self.sem, 1)

    def wait(self):
        self.engine.wait_ge(self.sem, self.base + self.n)

    def __call__(self, instruction):
        self.later(instruction)
        self.wait()


def block_kernel(nc, x, w_qkv, w_out, b_out, gamma, beta, theta, phi, theta_noise, phi_noise, out):
    x_v = x.rearrange("o (p t) d -> p (o t) d", p=P)
    out_v = out.rearrange("o (p t) d -> p (o t) d", p=P)
    ctx = ExitStack()
    with ctx:
        def sb(name, shape, dt=F32):
            return ctx.enter_context(nc.sbuf_tensor(name, shape, dt))

        def sem(name):
            return ctx.enter_context(nc.semaphore(name))

        ident = sb("ident", [P, P])
        x_sb = sb("x_sb", [P, NT, D])
        xn = sb("xn", [P, NT, D])
        x_beta = sb("x_beta", [P, NT, D])
        xT = sb("xT", [P, NT * P])
        wqkv_sb = sb("wqkv_sb", [P, 3 * D])
        w3 = sb("w3", [P, 3, D])
        wout_sb = sb("wout_sb", [P, D])
        bout_b = sb("bout_b", [P, D])
        gamma_b = sb("gamma_b", [P, D])
        beta_b = sb("beta_b", [P, D])
        k_hi = sb("k_hi", [P, S], F32R)
        k_lo = sb("k_lo", [P, S], F32R)
        q_hi = sb("q_hi", [P, S], F32R)
        q_lo = sb("q_lo", [P, S], F32R)
        k_rep = sb("k_rep", [P, G, S], F32R)
        q_rep = sb("q_rep", [P, G, CW], F32R)
        v_sb = sb("v_sb", [P, NT, H, VW])
        w_buf = sb("w_buf", [P, W_STEPS, HPG, CW])
        pv_sb = sb("pv_sb", [P, CW])
        den = sb("den", [P, TPC, HPG])
        o_sb = sb("o_sb", [P, TPC, D])
        oT = sb("oT", [P, CW])
        y = sb("y", [P, TPC, D])
        x1 = sb("x1", [P, TPC, D])
        x1T = sb("x1T", [P, CW])
        sq = sb("sq", [P, TPC, 2, D])
        mag = sb("mag", [P, TPC, D])
        x2 = sb("x2", [P, TPC, D])
        angles = sb("angles", [P, 4, D])
        turns = sb("turns", [P, 2, D])
        ffn_w = sb("ffn_w", [P, 2, D])
        averager = sb("averager", [P, P])
        stats = sb("stats", [P, NT, 6])
        mv = sb("mv", [P, NT, 2])
        inv_var = sb("inv_var", [P, NT])
        rstd = sb("rstd", [P, NT])
        stats_p = sb("stats_p", [P, TPC, 6])
        mv_p = sb("mv_p", [P, TPC, 2])
        iv_p = sb("iv_p", [P, 2, TPC])
        spare = sb("spare", [P, 1])
        spare_act = sb("spare_act", [P, 1])
        rs_p = sb("rs_p", [P, TPC])

        sc = [ctx.enter_context(nc.psum_tensor(f"sc{i}", [P, 2, CW], F32)) for i in range(PSUM_PAIRS)]
        pv = [ctx.enter_context(nc.psum_tensor(f"pv{i}", [P, CW], F32)) for i in range(2)]

        xT_bank = [sc[0][:, 0, :], sc[0][:, 1, :], pv[1][:, :], pv[1][:, :]]
        k_bank = [sc[1][:, 0, :], sc[1][:, 1, :], pv[1][:, :], pv[1][:, :]]
        v_bank = [sc[2][:, 0, :], pv[0][:, :], pv[1][:, :], pv[1][:, :]]
        q_bank = [pv[0][:, :], pv[0][:, :], pv[1][:, :], pv[0][:, :]]

        x_loaded = [sem(f"x_loaded{c}") for c in range(NC)]
        wqkv_loaded = sem("wqkv_loaded")
        consts_loaded = sem("consts_loaded")
        angles_loaded = sem("angles_loaded")
        ident_zero = sem("ident_zero")
        ident_ready = sem("ident_ready")
        w3_ready = sem("w3_ready")
        v_pad = sem("v_pad")
        ln_own = sem("ln_own")
        var_ready = sem("var_ready")
        rstd_ready = sem("rstd_ready")
        centred = sem("centred")
        xn_ready = sem("xn_ready")
        xT_done = sem("xT_done")
        xT_ready = sem("xT_ready")
        k_done = sem("k_done")
        q_done = sem("q_done")
        v_done = sem("v_done")
        k_hi_ready = sem("k_hi_ready")
        k_lo_ready = sem("k_lo_ready")
        q_hi_ready = sem("q_hi_ready")
        q_lo_ready = sem("q_lo_ready")
        v_ready = sem("v_ready")
        k0_loaded = [sem(f"k0_loaded{c}") for c in range(NC)]
        k_loaded = [None] + [sem(f"k_loaded{g}") for g in range(1, G)]
        q_first = sem("q_first")
        q_loaded = [sem(f"q_loaded{g}") for g in range(G)]
        x_centred = sem("x_centred")
        xb_ready = sem("xb_ready")
        trig_own = sem("trig_own")
        angles_ready = sem("angles_ready")
        averager_ready = sem("averager_ready")
        trig_done = sem("trig_done")
        means_done = sem("means_done")
        ffn_w_ready = sem("ffn_w_ready")
        scores = [sem("scores_act"), sem("scores_dve")]
        relu = [sem("relu_act"), sem("relu_dve")]
        pv_done = sem("pv_done")
        pv_out = sem("pv_out")
        pvT_done = sem("pvT_done")
        norm_own = sem("norm_own")
        normed = sem("normed")
        oT_done = sem("oT_done")
        oT_ready = sem("oT_ready")
        proj_done = sem("proj_done")
        y_ready = sem("y_ready")
        post_own = [sem("post_own0"), sem("post_own1")]
        iv_ready = [sem("iv_ready0"), sem("iv_ready1")]
        rs_ready = sem("rs_ready")
        x1_ready = sem("x1_ready")
        mean_back = sem("mean_back")
        x1T_done = sem("x1T_done")
        x1T_ready = sem("x1T_ready")
        ffn_done = sem("ffn_done")
        sq_ready = sem("sq_ready")
        sum_ready = sem("sum_ready")
        mag_ready = sem("mag_ready")
        x2_ready = sem("x2_ready")
        stored = sem("stored")

        def chunk(c):
            return bass.ds(c * TPC, TPC)

        class Part:

            def __init__(self, j, half=None):
                self.j, self.half = j, half
                self.n = j if half is None else j + half
                self.lo, self.tiles = (0, TPC) if half is None else (2 * half, 2)
                self.own = (post_own[half or 0], POST_SEQ * (0 if half else j))
                if half is None:
                    self.o_bank = self.y_bank = pv[1]
                    self.x1_bank = pv[0]
                else:
                    self.pv_bank, self.o_bank = sc[half][:, 0, :], sc[half][:, 1, :]
                    self.y_bank = sc[2][:, half, :]
                    self.x1_bank = self.pv_bank

            def sl(self):
                return slice(self.lo, self.lo + self.tiles)

            def cols(self):
                return slice(self.lo * P, (self.lo + self.tiles) * P)

            def all(self):
                return range(self.lo, self.lo + self.tiles)

            def rows(self):
                return bass.ds(self.j * TPC + self.lo, self.tiles)

            def pieces(self):
                if self.half is None:
                    return [(2 * self.j + i, range(2 * i, 2 * i + 2), pv[0]) for i in range(2)]
                return [(2 * (self.j + self.half) + i, range(self.lo + i, self.lo + i + 1), bank)
                        for i, bank in enumerate((self.o_bank, self.y_bank))]

        def row(v, d):
            return v[:, :].unsqueeze(1).to_broadcast([P, d, D])

        with nc.Block() as block:
            @block.sync
            def _(sp):
                def replicate_q(c, g):
                    for j in range(4):
                        src = q_lo if j % 2 else q_hi
                        sp.dma_start(
                            q_rep[j:P:4, g, :].bitcast(F32),
                            src[32 * g:32 * g + 32, bass.ds(c * CW, CW)].bitcast(F32),
                        ).then_inc(q_loaded[g], 16)

                def replicate_k(g, lo, n, done, parts=range(4)):
                    for j in parts:
                        src = k_lo if j // 2 else k_hi
                        sp.dma_start(
                            k_rep[j:P:4, g, lo:lo + n].bitcast(F32),
                            src[32 * g:32 * g + 32, lo:lo + n].bitcast(F32),
                        ).then_inc(done, 16)

                def store(part):
                    sp.wait_ge(x2_ready, part.n + 1 if part.half is None else part.j + 2 * part.half + 2)
                    sp.dma_start(out_v[:, part.rows(), :], x2[:, part.sl(), :]).then_inc(stored, 16)

                def next_queries(c, g):
                    if isinstance(c, int):
                        sp.wait_ge(q_lo_ready, c + 2)
                    for s in scores:
                        sp.wait_ge(s, STEPS * c + NT * (g + 1))
                    replicate_q(c + 1, g)

                sp.dma_start(x_sb[:, 0:TPC, :], x_v[:, 0:TPC, :]).then_inc(x_loaded[0], 16)
                sp.dma_start(wqkv_sb[:, :], w_qkv).then_inc(wqkv_loaded, 16)
                for c in range(1, NC):
                    sp.dma_start(x_sb[:, chunk(c), :], x_v[:, chunk(c), :]).then_inc(x_loaded[c], 16)
                for dst, src in ((bout_b, b_out), (gamma_b, gamma), (beta_b, beta)):
                    sp.dma_start(dst[:, :], src.partition_broadcast(P)).then_inc(consts_loaded, 16)
                sp.dma_start(wout_sb[:, :], w_out).then_inc(consts_loaded, 16)
                for n, src in enumerate((theta, phi, theta_noise, phi_noise)):
                    sp.dma_start(angles[:, n, :], src).then_inc(angles_loaded, 16)
                for c in range(NC):
                    sp.wait_ge(k_hi_ready, c + 1)
                    replicate_k(0, c * CW, CW, k0_loaded[c], (0, 1))
                    sp.wait_ge(k_lo_ready, c + 1)
                    replicate_k(0, c * CW, CW, k0_loaded[c], (2, 3))
                    if c == 0:
                        sp.wait_ge(q_lo_ready, 1)
                        for j in (1, 3):
                            sp.dma_start(q_rep[j:P:4, 0, :].bitcast(F32),
                                         q_lo[0:32, 0:CW].bitcast(F32)).then_inc(q_loaded[0], 16)
                for g in range(1, G):
                    replicate_q(0, g)
                    replicate_k(g, 0, S, k_loaded[g])

                for g in range(G):
                    next_queries(0, g)
                with sp.Fori(1, NC - 1) as c:
                    next_queries(c, 0)
                    next_queries(c, 1)
                    store(Part(c - 1))
                    next_queries(c, 2)
                    next_queries(c, 3)
                store(Part(NC - 2))
                store(Part(NC - 1, 0))
                store(Part(NC - 1, 1))
                sp.wait_ge(stored, 16 * (NC + 1))

            @block.gpsimd
            def _(pool):
                nc.gpsimd.memset(ident[:, :], 0.0).then_inc(ident_zero, 1)
                pool.wait_ge(ident_zero, 1)
                nc.gpsimd.affine_select(out=ident[:, :], in_=ident[:, :], compare_op=ALU.not_equal, fill=1.0,
                                        base=0, pattern=[[-1, P]], channel_multiplier=1).then_inc(ident_ready, 1)
                pool.wait_ge(wqkv_loaded, 16)
                for n in range(3):
                    src = wqkv_sb[:, :].rearrange("p (h c d) -> p c h d", h=H, c=3)[:, n]
                    nc.gpsimd.tensor_copy(w3[:, n, :].rearrange("p (h d) -> p h d", h=H), src).then_inc(w3_ready, 1)

                def pad_v(g):
                    heads = slice(HPG * g, HPG * (g + 1))
                    nc.gpsimd.memset(v_sb[:, :, heads, HD + 1:VW], 0.0).then_inc(v_pad, 1)
                    nc.gpsimd.memset(v_sb[:, :, heads, HD:HD + 1], 1.0).then_inc(v_pad, 1)

                def means(c):
                    return mv[:, chunk(c), 0:1].to_broadcast([P, TPC, D])

                def normalise_x(c):
                    pool.wait_ge(rstd_ready, c + 1)
                    nc.gpsimd.tensor_tensor(xn[:, chunk(c), :], x_sb[:, chunk(c), :],
                                            means(c), ALU.subtract).then_inc(centred, 1)
                    pool.wait_ge(centred, c)
                    nc.gpsimd.tensor_tensor(xn[:, chunk(c), :], xn[:, chunk(c), :],
                                            rstd[:, chunk(c)].unsqueeze(2).to_broadcast([P, TPC, D]),
                                            ALU.mult).then_inc(xn_ready, 1)

                pad_v(0)
                normalise_x(1)
                pool.wait_ge(q_hi_ready, 1)
                for j in (0, 2):
                    pool.dma_start(q_rep[j:P:4, 0, :].bitcast(F32), q_hi[0:32, 0:CW].bitcast(F32)).then_inc(q_first, 16)
                normalise_x(2)
                normalise_x(3)
                for g in range(1, G):
                    pad_v(g)
                nc.gpsimd.memset(averager[:, :], 1 / D).then_inc(averager_ready, 1)
                for c in range(NC):
                    nc.gpsimd.tensor_tensor(x_beta[:, chunk(c), :], x_sb[:, chunk(c), :], means(c),
                                            ALU.subtract).then_inc(x_centred, 1)
                pool.wait_ge(consts_loaded, 64)
                pool.wait_ge(xn_ready, NC)
                pool.wait_ge(xT_done, NC)
                for c in range(NC):
                    nc.gpsimd.tensor_tensor(xn[:, chunk(c), :], xn[:, chunk(c), :], row(bout_b, TPC),
                                            ALU.add).then_inc(xb_ready, 1)
                    pool.wait_ge(x_centred, c + 1)
                    nc.gpsimd.tensor_tensor(x_beta[:, chunk(c), :], x_beta[:, chunk(c), :], row(beta_b, TPC),
                                            ALU.add).then_inc(xb_ready, 1)

                def mean_again(part):
                    pool.wait_ge(x1_ready, part.n + 1)
                    nc.gpsimd.tensor_tensor(x2[:, part.sl(), :], x1[:, part.sl(), :],
                                            mv[:, part.rows(), 0:1].to_broadcast([P, part.tiles, D]),
                                            ALU.add).then_inc(mean_back, 1)

                def finish(part):
                    mean_again(part)
                    for n, tiles, _ in part.pieces():
                        sl = slice(tiles.start, tiles.stop)
                        pool.wait_ge(sq_ready, n + 1)
                        nc.gpsimd.tensor_tensor(mag[:, sl, :], sq[:, sl, 0, :], sq[:, sl, 1, :],
                                                ALU.add).then_inc(sum_ready, 1)
                    pool.wait_ge(mag_ready, 2 * part.n + 2)
                    pool.wait_ge(mean_back, part.n + 1)
                    nc.gpsimd.tensor_tensor(x2[:, :, :], x2[:, :, :], mag[:, :, :], ALU.add).then_inc(x2_ready, 1)

                finish(Part(0))
                with pool.Fori(1, NC - 1) as c:
                    pool.wait_ge(x2_ready, c)
                    pool.wait_ge(stored, 16 * c)
                    finish(Part(c))
                pool.wait_ge(x2_ready, NC - 1)
                pool.wait_ge(stored, 16 * (NC - 1))
                for half in range(2):
                    mean_again(Part(NC - 1, half))

            @block.scalar
            def _(act):
                def root(c):
                    act.wait_ge(var_ready, c + 1)
                    nc.scalar.activation(rstd[:, chunk(c)], inv_var[:, chunk(c)], ACT.Sqrt).then_inc(rstd_ready, 1)

                def take_xT(c):
                    act.wait_ge(xT_done, c + 1)
                    nc.scalar.copy(xT[:, c * CW:(c + 1) * CW], xT_bank[c]).then_inc(xT_ready, 1)

                def take_k(c):
                    act.wait_ge(k_done, c + 1)
                    nc.scalar.copy(k_hi[:, c * CW:(c + 1) * CW], k_bank[c]).then_inc(k_hi_ready, 1)

                def take_q(c):
                    act.wait_ge(q_done, c + 1)
                    nc.scalar.copy(q_hi[:, c * CW:(c + 1) * CW], q_bank[c]).then_inc(q_hi_ready, 1)

                def take_v(c):
                    act.wait_ge(v_done, c + 1)
                    nc.scalar.copy(v_sb[:, chunk(c), :, 0:HD],
                                   v_bank[c].rearrange("p (t h d) -> p t h d", t=TPC, h=H)).then_inc(v_ready, 1)

                root(0)
                take_xT(0)
                root(1)
                take_k(0)
                take_q(0)
                root(2)
                take_xT(1)
                take_v(0)
                take_k(1)
                root(3)

                def relu_step(c, s):
                    act.wait_ge(scores[0], STEPS * c + s + 1)
                    nc.scalar.activation(w_buf[:, s % W_STEPS, 0:2, :], sc[2 * s % PSUM_PAIRS][:, :, :],
                                         ACT.Relu).then_inc(relu[0], 1)

                def take_pv(m, bank):
                    act.wait_ge(pv_done, m + 1)
                    if not isinstance(m, int) or m > 0:
                        act.wait_ge(pvT_done, m)
                    nc.scalar.copy(pv_sb[:, :], bank[:, :]).then_inc(pv_out, 1)

                def trig():
                    act.wait_ge(angles_ready, 1)
                    nc.scalar.activation(ffn_w[:, :, :], angles[:, 0:2, :], ACT.Sin).then_inc(trig_done, 1)

                def sqrt_table():
                    nc.scalar.activation(spare_act[:, :], rstd[:, 0:1], ACT.Sqrt)

                def take_oT(part):
                    act.wait_ge(oT_done, part.n + 1)
                    nc.scalar.copy(oT[:, part.cols()], part.o_bank[:, 0:part.tiles * P]).then_inc(oT_ready, 1)

                def post_root(part):
                    act.wait_ge(iv_ready[0], part.n + 1)
                    nc.scalar.activation(rs_p[:, part.sl()], iv_p[:, 0, part.sl()], ACT.Sqrt).then_inc(rs_ready, 1)

                def take_x1T(part):
                    act.wait_ge(x1T_done, part.n + 1)
                    nc.scalar.copy(x1T[:, part.cols()], part.x1_bank[:, 0:part.tiles * P]).then_inc(x1T_ready, 1)

                def square(part, i):
                    n, tiles, bank = part.pieces()[i]
                    act.wait_ge(ffn_done, n + 1)
                    nc.scalar.activation(sq[:, tiles.start:tiles.stop, :, :].rearrange("p t c d -> p (t c d)"),
                                         bank[:, 0:len(tiles) * 2 * D], ACT.Square).then_inc(sq_ready, 1)

                def magnitude(part, i):
                    n, tiles, _ = part.pieces()[i]
                    if i == 0:
                        act.wait_ge(iv_ready[1], part.n + 1)
                    act.wait_ge(sum_ready, n + 1)
                    for t in tiles:
                        last = nc.scalar.activation(mag[:, t, :], mag[:, t, :], ACT.Sqrt, scale=iv_p[:, 1, t:t + 1])
                    last.then_inc(mag_ready, 1)

                def after_pass(j):
                    part = Part(j)
                    return [((0, 6), lambda: take_oT(part)), ((0, 12), lambda: post_root(part)),
                            ((1, 5), lambda: take_x1T(part)),
                            ((1, 7), lambda: square(part, 0)), ((1, 9), lambda: square(part, 1)),
                            ((1, 11), lambda: magnitude(part, 0)), ((1, 13), lambda: magnitude(part, 1))]

                def run_pass(c, hooks):
                    for g in range(G):
                        for k in range(NT):
                            relu_step(c, NT * g + k)
                            if k == 1 and not (isinstance(c, int) and c == 0 and g == 0):
                                take_pv(G * c + g - 1, pv[(g + 1) % 2])
                            for at, hook in hooks:
                                if at == (g, k):
                                    hook()

                run_pass(0, [((0, 0), lambda: take_v(1)), ((0, 0), lambda: take_xT(2)), ((0, 2), lambda: take_xT(3)),
                             ((0, 4), lambda: take_k(2)), ((0, 6), lambda: take_k(3)),
                             ((0, 8), lambda: take_v(2)), ((0, 10), lambda: take_v(3)),
                             ((1, 8), lambda: take_q(1)), ((2, 8), lambda: take_q(2)),
                             ((3, 8), lambda: take_q(3)), ((2, 12), trig), ((3, 3), sqrt_table)])
                with act.Fori(1, NC) as c:
                    run_pass(c, after_pass(c - 1))
                halves = [Part(NC - 1, 0), Part(NC - 1, 1)]
                act.wait_ge(pv_done, G * NC)
                act.wait_ge(pvT_done, G * NC - 1)
                for part in halves:
                    nc.scalar.copy(pv_sb[:, part.cols()], pv[1][:, part.cols()]).then_inc(pv_out, 1)
                for stage in (take_oT, post_root, take_x1T):
                    for part in halves:
                        stage(part)
                for stage in (square, magnitude):
                    for part in halves:
                        stage(part, 0)
                        stage(part, 1)

            @block.vector
            def _(dve):
                own = Own(dve, ln_own)

                def statistics(c):
                    dve.wait_ge(x_loaded[c], 16)
                    for t in range(c * TPC, (c + 1) * TPC):
                        last = nc.vector.bn_stats(stats[:, t, :], x_sb[:, t, :])
                    own(last)
                    for t in range(c * TPC, (c + 1) * TPC):
                        last = nc.vector.bn_aggr(mv[:, t, :], stats[:, t, :])
                    own(last)
                    own(nc.vector.tensor_scalar_add(inv_var[:, chunk(c)], mv[:, chunk(c), 1], LN_EPS))
                    nc.vector.reciprocal(inv_var[:, chunk(c)], inv_var[:, chunk(c)]).then_inc(var_ready, 1)

                def normalise_x(c):
                    dve.wait_ge(rstd_ready, c + 1)
                    for t in range(c * TPC, (c + 1) * TPC):
                        last = nc.vector.tensor_scalar(xn[:, t, :], x_sb[:, t, :], mv[:, t, 0:1], rstd[:, t:t + 1],
                                                       ALU.subtract, ALU.mult)
                    last.then_inc(xn_ready, 1)

                def low_part(lo, hi, hi_ready, lo_ready, c, bank):
                    cols = slice(c * CW, (c + 1) * CW)
                    dve.wait_ge(hi_ready, c + 1)
                    nc.vector.tensor_tensor(lo[:, cols], bank, hi[:, cols].bitcast(F32),
                                            ALU.subtract).then_inc(lo_ready, 1)

                def take_k(c):
                    low_part(k_lo, k_hi, k_hi_ready, k_lo_ready, c, k_bank[c])

                def take_q(c):
                    low_part(q_lo, q_hi, q_hi_ready, q_lo_ready, c, q_bank[c])

                statistics(0)
                normalise_x(0)
                statistics(1)
                statistics(2)
                take_k(0)
                take_q(0)
                statistics(3)
                take_k(1)

                def relu_step(c, s):
                    dve.wait_ge(scores[1], STEPS * c + s + 1)
                    nc.vector.tensor_scalar(w_buf[:, s % W_STEPS, 2:4, :], sc[(2 * s + 1) % PSUM_PAIRS][:, :, :],
                                            0.0, None, ALU.max).then_inc(relu[1], 1)

                def normalise(m, bank, g, tiles=slice(0, TPC), c=None):
                    own = Own(dve, norm_own, NORM_SEQ * m)
                    n = tiles.stop - tiles.start
                    pvT = bank[:, 0:n * P].rearrange("p (t i v) -> p t i v", t=n, i=HPG)
                    dve.wait_ge(pvT_done, m + 1)
                    own(nc.vector.tensor_scalar_add(den[:, tiles, :], pvT[:, :, :, HD], DEN_EPS))
                    own(nc.vector.reciprocal(den[:, tiles, :], den[:, tiles, :]))
                    if g == 0 and not isinstance(c, int):
                        dve.wait_ge(oT_done, c)
                    nc.vector.tensor_tensor(
                        o_sb[:, tiles, 32 * g:32 * g + 32].rearrange("p t (i d) -> p t i d", i=HPG),
                        pvT[:, :, :, 0:HD], den[:, tiles, :].unsqueeze(3).to_broadcast([P, n, HPG, HD]),
                        ALU.mult).then_inc(normed, 1)

                def trig_angles(own):
                    both = angles[:, 0:2, :]

                    def add_noise():
                        dve.wait_ge(angles_loaded, 64)
                        own(nc.vector.tensor_tensor(both, both, angles[:, 2:4, :], ALU.add))

                    def in_turns():
                        nc.vector.tensor_scalar(turns[:, 0, :], angles[:, 0, :], 1 / TWO_PI, 0.25, ALU.mult, ALU.add)
                        own(nc.vector.tensor_scalar(turns[:, 1, :], angles[:, 1, :], 1 / TWO_PI, None, ALU.mult))

                    def whole_turns():
                        own(nc.vector.tensor_scalar_add(turns[:, :, :], turns[:, :, :], ROUND))
                        own(nc.vector.tensor_scalar_add(turns[:, :, :], turns[:, :, :], -ROUND))

                    def subtract(part):
                        own(nc.vector.scalar_tensor_tensor(out=both, in0=turns[:, :, :], scalar=-part, in1=both,
                                                           op0=ALU.mult, op1=ALU.add))

                    def clamp():
                        own(nc.vector.tensor_scalar_add(angles[:, 0, :], angles[:, 0, :], math.pi / 2))
                        nc.vector.tensor_scalar(both, both, PI_BELOW, -PI_BELOW, ALU.min,
                                                ALU.max).then_inc(angles_ready, 1)

                    return [add_noise, in_turns, whole_turns,
                            *(lambda part=part: subtract(part) for part in TWO_PI_PARTS), clamp]

                def residual(part):
                    dve.wait_ge(proj_done, part.n + 1)
                    nc.vector.tensor_tensor(
                        y[:, part.sl(), :],
                        part.y_bank[:, 0:part.tiles * P].rearrange("p (t d) -> p t d", t=part.tiles),
                        xn[:, part.rows(), :], ALU.add).then_inc(y_ready, 1)
                    dve.wait_ge(y_ready, part.n + 1)

                def post_stats(part, src):
                    for t in part.all():
                        last = nc.vector.bn_stats(stats_p[:, t, :], src[:, t, :])
                    part.chain(last)

                def post_inverse(part, norm):
                    nc.vector.memset(spare[:, :], 0.0)
                    for t in part.all():
                        last = nc.vector.bn_aggr(mv_p[:, t, :], stats_p[:, t, :])
                    part.chain(last)
                    part.chain(nc.vector.tensor_scalar_add(iv_p[:, norm, part.sl()], mv_p[:, part.sl(), 1], LN_EPS))
                    nc.vector.reciprocal(iv_p[:, norm, part.sl()],
                                         iv_p[:, norm, part.sl()]).then_inc(iv_ready[norm], 1)

                def times_gamma(part):
                    for t in part.all():
                        last = nc.vector.scalar_tensor_tensor(out=y[:, t, :], in0=y[:, t, :], scalar=mv_p[:, t, 0:1],
                                                              in1=gamma_b[:, :], op0=ALU.subtract, op1=ALU.mult)
                    part.chain.later(last)

                def first_residual(part):
                    dve.wait_ge(rs_ready, part.n + 1)
                    part.chain.wait()
                    for t in part.all():
                        last = nc.vector.scalar_tensor_tensor(
                            out=x1[:, t, :], in0=y[:, t, :], scalar=rs_p[:, t:t + 1],
                            in1=x_beta[:, bass.ds(part.j * TPC + t, 1), :].rearrange("p o d -> p (o d)"),
                            op0=ALU.mult, op1=ALU.add)
                    last.then_inc(x1_ready, 1)
                    dve.wait_ge(x1_ready, part.n + 1)

                def centre_ffn_w():
                    dve.wait_ge(means_done, 1)
                    both = ffn_w[:, :, :].rearrange("p c d -> p (c d)")
                    nc.vector.tensor_tensor(both, both, pv[0][:, 0:2 * D], ALU.subtract).then_inc(ffn_w_ready, 1)

                def start_chain(part):
                    part.chain = Own(dve, *part.own)
                    return part

                def after_pass(j):
                    part = start_chain(Part(j))
                    return [((0, 8), lambda: residual(part)), ((0, 9), lambda: post_stats(part, y)),
                            ((0, 10), lambda: post_inverse(part, 0)), ((0, 11), lambda: times_gamma(part)),
                            ((0, 13), lambda: first_residual(part)), ((0, 14), lambda: post_stats(part, x1)),
                            ((1, 1), lambda: post_inverse(part, 1)),
                            ((3, 0), lambda: dve.wait_ge(x2_ready, part.n + 1))]

                def run_pass(c, hooks):
                    for g in range(G):
                        for k in range(NT):
                            relu_step(c, NT * g + k)
                            if k == 3 and not (isinstance(c, int) and c == 0 and g == 0):
                                normalise(G * c + g - 1, pv[(g + 1) % 2], (g - 1) % G, c=c)
                            for at, hook in hooks:
                                if at == (g, k):
                                    hook()

                own = Own(dve, trig_own)
                run_pass(0, [((0, 4), lambda: take_k(2)), ((0, 6), lambda: take_k(3)),
                             ((1, 8), lambda: take_q(1)), ((2, 8), lambda: take_q(2)),
                             ((3, 8), lambda: take_q(3)), ((3, 13), centre_ffn_w)]
                         + [((1 + n // 8, 9 + n % 8 if n < 7 else n - 7), part)
                            for n, part in enumerate(trig_angles(own))])
                dve.wait_ge(xb_ready, 2 * NC)
                dve.wait_ge(consts_loaded, 64)
                with dve.Fori(1, NC) as c:
                    run_pass(c, after_pass(c - 1))
                halves = [start_chain(Part(NC - 1, 0)), start_chain(Part(NC - 1, 1))]

                def tail_sum(part, i):
                    n, (t,), _ = part.pieces()[i]
                    dve.wait_ge(sq_ready, n + 1)
                    nc.vector.tensor_tensor(mag[:, t, :], sq[:, t, 0, :], sq[:, t, 1, :],
                                            ALU.add).then_inc(sum_ready, 1)

                def tail_finish(part, i):
                    n, (t,), _ = part.pieces()[i]
                    if i == 0:
                        dve.wait_ge(mean_back, part.n + 1)
                    dve.wait_ge(mag_ready, n + 1)
                    nc.vector.tensor_tensor(x2[:, t, :], x2[:, t, :], mag[:, t, :], ALU.add).then_inc(x2_ready, 1)

                for part in halves:
                    normalise(G * NC - 1 + part.half, part.pv_bank, G - 1, part.sl())
                for stage in (residual, lambda p: post_stats(p, y), lambda p: post_inverse(p, 0), times_gamma,
                              first_residual, lambda p: post_stats(p, x1), lambda p: post_inverse(p, 1)):
                    for part in halves:
                        stage(part)
                dve.wait_ge(x2_ready, NC - 1)
                for stage in (tail_sum, tail_finish):
                    for part in halves:
                        stage(part, 0)
                        stage(part, 1)

            @block.tensor
            def _(pe):
                def transpose_x(c):
                    pe.wait_ge(xn_ready, c + 1)
                    if c == 3:
                        pe.wait_ge(xT_ready, 3)
                    for t in range(TPC):
                        last = nc.tensor.transpose(xT_bank[c][:, t * P:(t + 1) * P], xn[:, c * TPC + t, :],
                                                   ident[:, :])
                    last.then_inc(xT_done, 1)

                def project_k(c):
                    if c == 2:
                        pe.wait_ge(xT_ready, 4)
                    elif c == 3:
                        pe.wait_ge(k_hi_ready, 3)
                        pe.wait_ge(k_lo_ready, 3)
                    else:
                        pe.wait_ge(xT_ready, c + 1)
                    nc.tensor.matmul(k_bank[c], w3[:, 1, :], xT[:, c * CW:(c + 1) * CW], start=True,
                                     stop=True).then_inc(k_done, 1)

                def project_q(c):
                    if c > 0:
                        pe.wait_ge(normed, c)
                    nc.tensor.matmul(q_bank[c], w3[:, 0, :], xT[:, c * CW:(c + 1) * CW], start=True,
                                     stop=True).then_inc(q_done, 1)

                def project_v(c):
                    if c == 2:
                        pe.wait_ge(k_hi_ready, 4)
                        pe.wait_ge(k_lo_ready, 4)
                    elif c == 3:
                        pe.wait_ge(v_ready, 3)
                    for t in range(TPC):
                        last = nc.tensor.matmul(v_bank[c][:, t * P:(t + 1) * P],
                                                xT[:, (c * TPC + t) * P:(c * TPC + t + 1) * P], w3[:, 2, :],
                                                start=True, stop=True)
                    last.then_inc(v_done, 1)

                def warm_up(n):
                    for _ in range(n):
                        nc.tensor.matmul(pv[0][:, 0:P], ident[:, :], ident[:, :], start=True, stop=True)

                pe.wait_ge(ident_ready, 1)
                warm_up(WARM_UP)
                transpose_x(0)
                pe.wait_ge(w3_ready, 3)
                project_k(0)
                project_q(0)
                project_v(0)
                transpose_x(1)
                project_k(1)
                pe.wait_ge(q_lo_ready, 1)
                warm_up(WARM_UP // 2)

                def score_step(c, s):
                    g, k = divmod(s, NT)
                    first = isinstance(c, int) and c == 0
                    if k == 0:
                        if first and g == 0:
                            pe.wait_ge(q_first, 32)
                            pe.wait_ge(q_loaded[0], 32)
                        else:
                            pe.wait_ge(q_loaded[g], 64 * (c + 1) - (32 if g == 0 else 0))
                    if first and g == 0 and k % TPC == 0:
                        pe.wait_ge(k0_loaded[k // TPC], 64)
                    if first and g > 0 and k == 0:
                        pe.wait_ge(k_loaded[g], 64)
                    for half in range(2):
                        pair = 2 * s + half
                        buf = pair % PSUM_PAIRS
                        if pair >= PSUM_PAIRS:
                            user, back = pair - PSUM_PAIRS, 0
                        else:
                            user, back = next(p for p in range(2 * STEPS - 1, 0, -1) if p % PSUM_PAIRS == buf), 1
                        if not (first and back):
                            pe.wait_ge(relu[user % 2], STEPS * (c - back) + user // 2 + 1)
                        elif buf == 0:
                            pe.wait_ge(xT_ready, 2)
                        elif buf == 1:
                            pe.wait_ge(k_hi_ready, 2)
                            pe.wait_ge(k_lo_ready, 2)
                        else:
                            pe.wait_ge(v_ready, 1)
                        for i in (2 * half, 2 * half + 1):
                            rows = slice(32 * i, 32 * i + 32)
                            last = nc.tensor.matmul(sc[buf][:, i % 2, :], k_rep[rows, g, k * P:(k + 1) * P],
                                                    q_rep[rows, g, :], start=True, stop=True)
                        last.then_inc(scores[half], 1)

                def value_step(c, s):
                    g, k = divmod(s, NT)
                    first = isinstance(c, int) and c == 0
                    bank = pv[g % 2]
                    if k == 0:
                        if first:
                            pe.wait_ge(v_pad, 2 * (g + 1))
                        if not first or g >= 2:
                            pe.wait_ge(normed, G * c + g - 1)
                        if first and g == 1:
                            pe.wait_ge(v_ready, NC)
                        if first and g >= 2:
                            pe.wait_ge(q_lo_ready, g)
                        if not first and g == 0:
                            pe.wait_ge(q_lo_ready, NC)
                        if not first and g == 1:
                            pe.wait_ge(y_ready, c)
                        if not first and g == 2:
                            pe.wait_ge(sq_ready, 2 * c)
                    if first and g == 0 and k % TPC == 0:
                        pe.wait_ge(v_ready, max(2, k // TPC + 1))
                    for i in (1, 2, 3, 0):
                        if i in (1, 2):
                            pe.wait_ge(relu[i // 2], STEPS * c + s + 1)
                        last = nc.tensor.matmul(bank[32 * i:32 * i + 32, :], v_sb[:, k, HPG * g + i, :],
                                                w_buf[:, s % W_STEPS, i, :], start=(k == 0), stop=(k == NT - 1))
                    if k == NT - 1:
                        last.then_inc(pv_done, 1)

                def transpose_tiles(bank, src, tiles, done):
                    for n, t in enumerate(tiles):
                        last = nc.tensor.transpose(bank[:, n * P:(n + 1) * P], src(t), ident[:, :])
                    last.then_inc(done, 1)

                def transpose_pv(m, bank, tiles=range(TPC)):
                    pe.wait_ge(pv_out, m + 1)
                    transpose_tiles(bank, lambda t: pv_sb[:, t * P:(t + 1) * P], tiles, pvT_done)

                def transpose_o(part):
                    pe.wait_ge(normed, G * part.j + G + (part.half or 0))
                    transpose_tiles(part.o_bank, lambda t: o_sb[:, t, :], part.all(), oT_done)

                def project_out(part):
                    pe.wait_ge(oT_ready, part.n + 1)
                    for n, t in enumerate(part.all()):
                        last = nc.tensor.matmul(part.y_bank[:, n * P:(n + 1) * P], oT[:, t * P:(t + 1) * P],
                                                wout_sb[:, :], start=True, stop=True)
                    last.then_inc(proj_done, 1)

                def transpose_x1(part):
                    pe.wait_ge(x1_ready, part.n + 1)
                    if part.half is None:
                        pe.wait_ge(normed, G * part.j + G + 1)
                    transpose_tiles(part.x1_bank, lambda t: x1[:, t, :], part.all(), x1T_done)

                def ffn_means():
                    pe.wait_ge(averager_ready, 1)
                    pe.wait_ge(trig_done, 1)
                    pe.wait_ge(q_hi_ready, NC)
                    pe.wait_ge(q_lo_ready, NC)
                    nc.tensor.matmul(pv[0][:, 0:2 * D], averager[:, :], ffn_w[:, :, :].rearrange("p c d -> p (c d)"),
                                     start=True, stop=True).then_inc(means_done, 1)

                def ffn(part, i):
                    n, tiles, bank = part.pieces()[i]
                    if i == 0:
                        pe.wait_ge(x1T_ready, part.n + 1)
                    elif part.half is None:
                        pe.wait_ge(sq_ready, n)
                    for m, t in enumerate(tiles):
                        last = nc.tensor.matmul(bank[:, m * 2 * D:(m + 1) * 2 * D], x1T[:, t * P:(t + 1) * P],
                                                ffn_w[:, :, :].rearrange("p c d -> p (c d)"), start=True, stop=True)
                    last.then_inc(ffn_done, 1)

                def after_pass(j):
                    part = Part(j)
                    return [((0, 5), lambda: transpose_o(part)), ((0, 7), lambda: project_out(part)),
                            ((1, 4), lambda: transpose_x1(part)), ((1, 6), lambda: ffn(part, 0)),
                            ((1, 8), lambda: ffn(part, 1))]

                def run_pass(c, hooks):
                    for s in range(STEPS):
                        score_step(c, s)
                        if s == 0:
                            if isinstance(c, int) and c == 0:
                                project_v(1)
                                transpose_x(2)
                            else:
                                value_step(c - 1, STEPS - 1)
                            continue
                        g, k = divmod(s - 1, NT)
                        if k == 2 and not (isinstance(c, int) and c == 0 and g == 0):
                            transpose_pv(G * c + g - 1, pv[(g + 1) % 2])
                        for at, hook in hooks:
                            if at == (g, k):
                                hook()
                        value_step(c, s - 1)

                run_pass(0, [((0, 1), lambda: transpose_x(3)), ((0, 3), lambda: project_k(2)),
                             ((0, 5), lambda: project_k(3)), ((0, 7), lambda: project_v(2)),
                             ((0, 9), lambda: project_v(3))]
                         + [((c, 7), lambda c=c: project_q(c)) for c in range(1, NC)] + [((3, 11), ffn_means)])
                pe.wait_ge(consts_loaded, 64)
                pe.wait_ge(ffn_w_ready, 1)
                with pe.Fori(1, NC) as c:
                    run_pass(c, after_pass(c - 1))
                value_step(NC - 1, STEPS - 1)
                halves = [Part(NC - 1, 0), Part(NC - 1, 1)]
                for part in halves:
                    transpose_pv(G * NC - 1 + part.half, part.pv_bank, part.all())
                for stage in (transpose_o, project_out):
                    for part in halves:
                        stage(part)
                warm_up(TAIL_WARM_UP)
                for part in halves:
                    transpose_x1(part)
                for part in halves:
                    ffn(part, 0)
                    ffn(part, 1)


_INS = ["x", "w_qkv", "w_out", "b_out", "gamma", "beta", "theta", "phi", "theta_noise", "phi_noise"]


def kernel(**inputs):
    import numpy as np
    import concourse.bacc as bacc
    from concourse.bass_utils import run_bass_kernel_spmd

    nc = bacc.Bacc("TRN2", target_bir_lowering=False, num_devices=1)
    arrays, args = {}, []
    for name in _INS:
        full = ("L0_attn_" if name in _INS[:6] else "L0_ffn_") + name
        a = np.ascontiguousarray(inputs[full])
        arrays[f"{name}_dram"] = a
        args.append(nc.dram_tensor(f"{name}_dram", a.shape, mybir.dt.from_np(a.dtype), kind="ExternalInput").ap())
    args.append(nc.dram_tensor("out_dram", (1, S, D), F32, kind="ExternalOutput").ap())
    block_kernel(nc, *args)
    r = run_bass_kernel_spmd(nc, [arrays], core_ids=[0])
    return r.results[0]["out_dram"]
```
